# Optimizing a Trainium2 kernel written in Bass

```python
import numpy as np
import jax
import jax.numpy as jnp

def _softmax(x, axis=-1):
    return jax.nn.softmax(x, axis=axis)

def _gelu(x):
    return jax.nn.gelu(x, approximate=True)

def _silu(x):
    return jax.nn.silu(x)

def _sigmoid(x):
    return jax.nn.sigmoid(x)

def _layernorm(x, axis=-1, eps=1e-05):
    m = jnp.mean(x, axis=axis, keepdims=True)
    v = jnp.var(x, axis=axis, keepdims=True)
    return (x - m) / jnp.sqrt(v + eps)

def _scatter_add(tgt, idx, src, axis=0):
    return tgt.at[idx].add(src)

def _segment_sum(src, seg, n):
    return jax.ops.segment_sum(src, seg, n)
kernel_name = 'mk_sandwich_d1_jaxref_r4_20619d'

def setup_inputs(seed: int=0):
    np.random.seed(seed)
    _w = jnp.asarray

    def _L0_attn_setup():
        import math
        import jax, jax.numpy as jnp
        import numpy as np
        B, S, D = (2, 512, 256)
        N_HEADS, D_KV = (16, 64)
        INNER = N_HEADS * D_KV
        NUM_BUCKETS = 32
        MAX_DISTANCE = 128

        def _relative_position_bucket(relative_position, num_buckets=NUM_BUCKETS, max_distance=MAX_DISTANCE):
            nb = num_buckets // 2
            rel_buckets = (relative_position > 0).astype(jnp.int32) * nb
            rp = jnp.abs(relative_position)
            max_exact = nb // 2
            is_small = rp < max_exact
            rp_safe = jnp.maximum(rp, 1)
            rp_if_large = max_exact + (jnp.log(rp_safe.astype(jnp.float32) / max_exact) / math.log(max_distance / max_exact) * (nb - max_exact)).astype(jnp.int32)
            rp_if_large = jnp.minimum(rp_if_large, nb - 1)
            return rel_buckets + jnp.where(is_small, rp, rp_if_large)

        def compute_bias(rel_bias, q_len, k_len):
            ctx = jnp.arange(q_len)[:, None]
            mem = jnp.arange(k_len)[None, :]
            buckets = _relative_position_bucket(mem - ctx)
            values = rel_bias[buckets]
            return jnp.transpose(values, (2, 0, 1))[None]
        key = jax.random.key(seed)
        ks = jax.random.split(key, 6)
        s = 1.0 / math.sqrt(D)
        return {'hidden_states': jax.random.normal(ks[0], (B, S, D), jnp.float32), 'wq': jax.random.normal(ks[1], (D, INNER), jnp.float32) * s, 'wk': jax.random.normal(ks[2], (D, INNER), jnp.float32) * s, 'wv': jax.random.normal(ks[3], (D, INNER), jnp.float32) * s, 'wo': jax.random.normal(ks[4], (INNER, D), jnp.float32) * s, 'rel_bias': jax.random.normal(ks[5], (NUM_BUCKETS, N_HEADS), jnp.float32) * 0.1}
    _L0_attn_in = _L0_attn_setup()

    def _L0_ffn_setup():
        import jax, jax.numpy as jnp
        import numpy as np
        NEG_INF = -1e+30
        K = 2
        key = jax.random.key(seed)
        ks = jax.random.split(key, 5)
        B, S, D, O, E = (8, 512, 256, 256, 8)
        scale = 1.0 / np.sqrt(D)
        return {'x': jax.random.normal(ks[0], (B, S, D), dtype=jnp.float32), 'gate_w': jax.random.normal(ks[1], (E, D), dtype=jnp.float32) * scale, 'gate_b': jnp.zeros((E,), dtype=jnp.float32), 'expert_w': jax.random.normal(ks[2], (E, O, D), dtype=jnp.float32) * scale, 'expert_b': jnp.zeros((E, O), dtype=jnp.float32)}
    _L0_ffn_in = _L0_ffn_setup()
    _d = {'L0_attn_hidden_states': _L0_attn_in['hidden_states'], 'L0_attn_wq': _L0_attn_in['wq'], 'L0_attn_wk': _L0_attn_in['wk'], 'L0_attn_wv': _L0_attn_in['wv'], 'L0_attn_wo': _L0_attn_in['wo'], 'L0_attn_rel_bias': _L0_attn_in['rel_bias'], 'L0_ffn_gate_w': _L0_ffn_in['gate_w'], 'L0_ffn_gate_b': _L0_ffn_in['gate_b'], 'L0_ffn_expert_w': _L0_ffn_in['expert_w'], 'L0_ffn_expert_b': _L0_ffn_in['expert_b']}
    _x0 = _d['L0_attn_hidden_states']
    _d['L0_attn_hidden_states'] = jax.random.normal(jax.random.fold_in(jax.random.key(seed), 1), (2, 2048, 256), dtype=_x0.dtype)
    del _x0
    return _d

def reference(L0_attn_hidden_states, L0_attn_wq, L0_attn_wk, L0_attn_wv, L0_attn_wo, L0_attn_rel_bias, L0_ffn_gate_w, L0_ffn_gate_b, L0_ffn_expert_w, L0_ffn_expert_b):

    def _L0_attn_ref(hidden_states, wq, wk, wv, wo, rel_bias):
        import math
        import jax, jax.numpy as jnp
        import numpy as np
        B, S, D = (2, 512, 256)
        N_HEADS, D_KV = (16, 64)
        INNER = N_HEADS * D_KV
        NUM_BUCKETS = 32
        MAX_DISTANCE = 128

        def _relative_position_bucket(relative_position, num_buckets=NUM_BUCKETS, max_distance=MAX_DISTANCE):
            nb = num_buckets // 2
            rel_buckets = (relative_position > 0).astype(jnp.int32) * nb
            rp = jnp.abs(relative_position)
            max_exact = nb // 2
            is_small = rp < max_exact
            rp_safe = jnp.maximum(rp, 1)
            rp_if_large = max_exact + (jnp.log(rp_safe.astype(jnp.float32) / max_exact) / math.log(max_distance / max_exact) * (nb - max_exact)).astype(jnp.int32)
            rp_if_large = jnp.minimum(rp_if_large, nb - 1)
            return rel_buckets + jnp.where(is_small, rp, rp_if_large)

        def compute_bias(rel_bias, q_len, k_len):
            ctx = jnp.arange(q_len)[:, None]
            mem = jnp.arange(k_len)[None, :]
            buckets = _relative_position_bucket(mem - ctx)
            values = rel_bias[buckets]
            return jnp.transpose(values, (2, 0, 1))[None]
        b, s, _ = hidden_states.shape

        def shape(x):
            return x.reshape(b, s, N_HEADS, D_KV).transpose(0, 2, 1, 3)
        q = shape(hidden_states @ wq)
        k = shape(hidden_states @ wk)
        v = shape(hidden_states @ wv)
        scores = jnp.einsum('bhqd,bhkd->bhqk', q, k)
        position_bias = compute_bias(rel_bias, s, s)
        scores = scores + position_bias
        attn = jax.nn.softmax(scores.astype(jnp.float32), axis=-1).astype(scores.dtype)
        out = jnp.einsum('bhqk,bhkd->bhqd', attn, v)
        out = out.transpose(0, 2, 1, 3).reshape(b, s, INNER)
        return out @ wo

    def _L0_ffn_ref(x, gate_w, gate_b, expert_w, expert_b):
        import jax, jax.numpy as jnp
        import numpy as np
        NEG_INF = -1e+30
        K = 2
        pooled = x.mean(axis=1)
        logits = pooled @ gate_w.T + gate_b
        topk_vals, _ = jax.lax.top_k(logits, K)
        min_topk = topk_vals[:, -1:]
        masked = jnp.where(logits < min_topk, -jnp.inf, logits)
        gates = jax.nn.softmax(masked, axis=-1)
        expert_out = jax.nn.gelu(jnp.einsum('bsd,eod->beso', x, expert_w) + expert_b[None, :, None, :], approximate=False)
        return jnp.einsum('be,beso->bso', gates, expert_out)
    x = L0_attn_hidden_states
    x = x + _layernorm(_L0_attn_ref(_layernorm(x, axis=-1), L0_attn_wq, L0_attn_wk, L0_attn_wv, L0_attn_wo, L0_attn_rel_bias), axis=-1)
    x = x + _layernorm(_L0_ffn_ref(_layernorm(x, axis=-1), L0_ffn_gate_w, L0_ffn_gate_b, L0_ffn_expert_w, L0_ffn_expert_b), axis=-1)
    return x

_drawn_inputs = setup_inputs


def setup_inputs(seed=0):
    import zlib

    import numpy as np

    out = dict(_drawn_inputs(seed))
    spreads = {'L0_ffn_gate_b': (0.0, 0.1), 'L0_ffn_expert_b': (0.0, 0.1)}
    factors = {'L0_attn_rel_bias': 3.224}
    for name, (base, spread) in spreads.items():
        noise = np.random.default_rng([zlib.crc32(name.encode()), seed]).standard_normal(out[name].shape)
        drawn = base * np.exp(spread * noise) if base else spread * noise
        out[name] = jnp.asarray(drawn.astype(out[name].dtype))
    for name, factor in factors.items():
        out[name] = (out[name] * factor).astype(out[name].dtype)
    return out
```

```python
import numpy as np
import concourse.bass as bass
from concourse import mybir
from contextlib import ExitStack

B, S, D = 2, 2048, 256
H, DK = 16, 64
PAIRS = H // 2
BUCKETS = 32
E = 8
KT = D // 128
TT = S // 128
QC = 512
CHUNKS = S // QC
QT = QC // 128
BAND = 3 * 128
EPS = 1e-5
M_UNIT = 256.0
STEPS = CHUNKS * TT
BUCKET_FROM = [0, 1, 2, 3, 4, 5, 6, 7, 8, 12, 16, 23, 32, 46, 64, 91]
BIAS_ROW = 64
MAX_ROW = 96


def key_tiles(c):
    near = [j for j in range(QT * c - 1, QT * c + QT + 1) if 0 <= j < TT]
    return [j for j in range(TT) if j not in near] + near


def band_span(c, j):
    lo, hi = max(128 * (j - 1), QC * c), min(128 * (j + 2), QC * (c + 1))
    return (lo - QC * c, hi - QC * c, lo - 128 * (j - 1)) if lo < hi else None


def pre_span(i, kc):
    lo, hi = max(128 * (i - 1), 512 * kc), min(128 * (i + 2), 512 * (kc + 1))
    return (lo - 512 * kc, hi - 512 * kc, lo - 128 * (i - 1)) if lo < hi else None


PIECES = QT * 2 * 4
PER_STEP = 3
LAST_PRE = (PIECES - 1) // PER_STEP
POOL_SUMS = LAST_PRE + 1
RING = 4


def pieces_of(s):
    return range(PER_STEP * s, min(PER_STEP * (s + 1), PIECES)) if s <= LAST_PRE else range(0)


def shape_tables():
    rp = np.arange(-255, 256)
    bucket = np.array([max(n for n in range(16) if BUCKET_FROM[n] <= abs(r)) + 16 * (r > 0) for r in rp])
    hot = (np.arange(BUCKETS)[:, None] == bucket[None, :]).astype(np.float32)
    onehot = np.zeros((BUCKETS, 2, 512), np.float32)
    onehot[:, 0, :511] = hot[:, ::-1]
    onehot[:, 1, :511] = hot
    rows = np.zeros((32, 3, TT), np.float32)
    r, j = np.arange(32)[:, None], np.arange(TT)[None, :]
    rows[:, 0] = j - r // 2 >= 2
    rows[:, 1] = j == r // 2
    rows[:, 2, 0] = np.arange(32) % 2 == 0
    rows[:, 2, 1] = np.arange(32) % 2 == 1
    return onehot, rows, np.eye(128, dtype=np.float32)


def layer(nc, x, wq, wk, wv, wo, rel_bias, gate_wT, gate_b, expert_wT, expert_bT, onehot, rows, eye, out, w_scratch, t_scratch):
    f32, f16 = mybir.dt.float32, mybir.dt.float16
    ACT, ALU, AX = mybir.ActivationFunctionType, mybir.AluOpType, mybir.AxisListType

    ctx = ExitStack()
    with ctx:
        def sb(name, shape, dt):
            return ctx.enter_context(nc.sbuf_tensor(name, shape, dt))

        def pb(name, shape, dt):
            return ctx.enter_context(nc.psum_tensor(name, shape, dt))

        def sem(name):
            return ctx.enter_context(nc.semaphore(name))

        xb = sb("xb", [128, TT, D], f32)
        xT = sb("xT", [128, KT, S], f32)
        q1 = sb("q1", [128, CHUNKS, 2, QC], f16)
        q2 = sb("q2", [128, CHUNKS, 2, QC], f16)
        k1 = sb("k1", [128, 2, S], f16)
        k2 = sb("k2", [128, 2, S], f16)
        v = sb("v", [128, TT, 128], f32)
        prob = sb("prob", [128, RING, 2, QC], f32)
        accv = sb("accv", [128, 2, QC], f32)
        accp = sb("accp", [128, 2, QC], f32)
        oT = sb("oT", [128, PAIRS, S], f32)
        rden = sb("rden", [128, QC], f32)
        t1 = sb("t1", [128, 2, BAND], f32)
        t2f = sb("t2f", [128, 2, BAND], f32)
        t2 = sb("t2", [128, 2, BAND], f16)
        w3 = sb("w3", [128, 3, KT, 128], f32)
        wo_s = sb("wo_s", [128, PAIRS, D], f32)
        ident = sb("ident", [128, 128], f32)
        ident16 = sb("ident16", [128, 128], f16)
        ones = sb("ones", [128, 128], f32)
        mpart = sb("mpart", [128, 2, QT, 4], f32)
        mcol = sb("mcol", [128, 2 * QT], f32)
        mrow = sb("mrow", [2 * QT, 128], f16)
        rowc = sb("rowc", [96, 3, TT], f32)
        far = sb("far", [96, 6, H], f32)
        fparity = sb("fparity", [96, H], f32)
        rb = sb("rb", [BUCKETS, 3, H], f32)
        hot = sb("hot", [BUCKETS, 2, 512], f32)
        wv_s = sb("wv_s", [H, 2, 512], f32)
        stats = sb("stats", [128, TT, 6], f32)
        mv = sb("mv", [128, TT, 2], f32)
        std = sb("std", [128, TT], f32)
        rstd = sb("rstd", [128, TT], f32)
        pooled = sb("pooled", [128, KT], f32)
        gwT = sb("gwT", [128, KT, E], f32)
        eb = sb("eb", [128, E * KT], f32)
        g1 = sb("g1", [1, 8, E], f32)
        gate = sb("gate", [128, E], f32)
        q1f = q1[:, :, :, :].rearrange("p c h q -> p (c h q)")
        yb = xT[:, :, :].rearrange("p k (a d) -> p (k a) d", d=D)
        xn = prob[:, :, :, :].rearrange("p r h q -> p r (h q)")
        ft = oT[:, 0:2, :].rearrange("p k (a d) -> p (k a) d", d=D)
        ewT = oT[:, 2:4, :]
        ge = prob[:, :, :, :].rearrange("p r h q -> p (r h) q")
        accf = [accv, accp]

        st = pb("st", [128, 4, 512], f32)
        pre = pb("pre", [128, 2, 512], f32)
        po = pb("po", [128, 512], f32)
        pm = pb("pm", [128, 512], f32)

        consts_in = sem("consts_in")
        rel_in = sem("rel_in")
        set_pool = sem("set_pool")
        set_v = sem("set_v")
        set_a = sem("set_a")
        set_pe = sem("set_pe")
        scratch_out = sem("scratch_out")
        tables_out = sem("tables_out")
        x_in = sem("x_in")
        x_free = sem("x_free")
        ew_in = sem("ew_in")
        w_in = sem("w_in")
        t_in = sem("t_in")
        t2_cast = sem("t2_cast")
        pair_free = sem("pair_free")
        fill = sem("fill")
        hi_a = sem("hi_a")
        lo_v = sem("lo_v")
        v_a = sem("v_a")
        far_set = sem("far_set")
        q_dup = sem("q_dup")
        k_dup = sem("k_dup")
        pre_ready = sem("pre_ready")
        pre_used = sem("pre_used")
        m_col = sem("m_col")
        m_tr = sem("m_tr")
        m_row = sem("m_row")
        m_in = sem("m_in")
        st_ready = sem("st_ready")
        band_in = sem("band_in")
        exp_done = sem("exp_done")
        pv_done = sem("pv_done")
        o_out = sem("o_out")
        sum_v = sem("sum_v")
        sum_p = sem("sum_p")
        acc_used = sem("acc_used")
        den_ready = sem("den_ready")
        rden_done = sem("rden_done")
        norm_done = sem("norm_done")
        m_read = sem("m_read")
        lnv = sem("lnv")
        ln_add = sem("ln_add")
        ln_sq = sem("ln_sq")
        xn_ready = sem("xn_ready")
        tr_ready = sem("tr_ready")
        xT_a = sem("xT_a")
        xT_v = sem("xT_v")
        wo_ready = sem("wo_ready")
        y_out = sem("y_out")
        res = sem("res")
        gv = sem("gv")
        g_log = sem("g_log")
        g_exp = sem("g_exp")
        g_bc = sem("g_bc")
        gate_set = sem("gate_set")
        ff_ready = sem("ff_ready")
        gelu_done = sem("gelu_done")
        ff_acc = sem("ff_acc")
        ft_ready = sem("ft_ready")
        ft_out = sem("ft_out")
        out_done = sem("out_done")

        block = ctx.enter_context(nc.Block())

        NBAND = sum(band_span(c, j) is not None for c in range(CHUNKS) for j in range(TT))
        VSUM = TT - POOL_SUMS - 1

        @block.sync
        def _(sp):
            sp.dma_start(ident[:, :], eye).then_inc(consts_in, 16)
            sp.dma_start(hot[:, :, :], onehot).then_inc(consts_in, 16)
            sp.dma_start(rowc[64:96, :, :], rows).then_inc(consts_in, 16)
            sp.dma_start(rb[:, 0, :], rel_bias).then_inc(rel_in, 16)
            sp.dma_start(rb[:, 1, :], rel_bias[15:16, :].broadcast_to((BUCKETS, H))).then_inc(rel_in, 16)
            sp.dma_start(far[64:96, 0, :], rel_bias[31:32, :].broadcast_to((32, H))).then_inc(rel_in, 16)
            sp.dma_start(far[64:96, 1, :], rel_bias[15:16, :].broadcast_to((32, H))).then_inc(rel_in, 16)
            sp.dma_start(wo_s[:, :, :], wo.rearrange("(a p) n -> p a n", p=128)).then_inc(consts_in, 16)
            sp.dma_start(gwT[:, :, :], gate_wT.rearrange("(k p) e -> p k e", p=128)).then_inc(consts_in, 16)
            sp.dma_start(eb[:, :], expert_bT).then_inc(consts_in, 16)
            sp.dma_start(g1[0:1, 0, :], gate_b).then_inc(consts_in, 16)
            sp.wait_ge(set_a, 2)
            sp.dma_start(w_scratch, wv_s[:, :, :]).then_inc(scratch_out, 16)
            sp.wait_ge(scratch_out, 16)
            for n in range(2):
                rows_of = w_scratch[:, n, 127:127 + BAND]
                rows_of = bass.AP(rows_of.tensor, rows_of.offset, [[1024, H], [-1, 128], [1, BAND]])
                sp.dma_start(t_scratch[n, :, :, :], rows_of).then_inc(tables_out, 16)
            sp.wait_ge(tables_out, 32)
            with sp.Fori(0, B) as b:
                sp.wait_ge(x_free, b + 1)
                sp.dma_start(xb[:, :, :], x[bass.ds(b, 1), :, :].rearrange("b (t p) d -> p (b t) d", p=128)).then_inc(x_in, 16)
                with sp.Fori(0, PAIRS) as hp:
                    pair = b * PAIRS + hp
                    sp.wait_ge(fill, pair * 12 + 1)
                    for n, w in enumerate((wq, wk, wv)):
                        sp.dma_start(w3[:, n, :, :], w[:, bass.ds(hp * 128, 128)].rearrange("(k p) c -> p k c", p=128)).then_inc(w_in, 16)
                    sp.wait_ge(pair_free, 2 * pair + 2)
                    for n, t in enumerate((t1, t2f)):
                        sp.dma_start(t[:, :, :], t_scratch[n, bass.ds(2 * hp, 2), :, :].rearrange("h p u -> p h u")).then_inc(t_in, 16)
                    sp.wait_ge(hi_a, pair * 16 + 8)
                    sp.dma_start(q2[0:64, :, :, :], q1[0:64, :, :, :]).then_inc(q_dup, 16)
                    sp.wait_ge(hi_a, pair * 16 + 16)
                    sp.dma_start(k2[64:128, :, :], k1[0:64, :, :]).then_inc(k_dup, 16)
                    for c in range(CHUNKS):
                        sp.wait_ge(m_row, pair * CHUNKS + c + 1)
                        sp.dma_start(q1[MAX_ROW:MAX_ROW + 1, c, :, :].rearrange("p h (t q) -> p (h t) q", q=128),
                                     mrow[:, :]).then_inc(m_in, 16)
                sp.wait_ge(wo_ready, b * TT + TT)
                sp.dma_start(ewT, expert_wT.rearrange("(k p) n -> p k n", p=128)).then_inc(ew_in, 16)
                sp.wait_ge(res, b * 2 * TT + 2 * TT)
                sp.dma_start(out[bass.ds(b, 1), :, :].rearrange("b (t p) d -> p (b t) d", p=128), xb[:, :, :]).then_inc(out_done, 16)
                sp.wait_ge(out_done, 16 * b + 16)
                sp.nop().then_inc(x_free, 1)

        @block.gpsimd
        def _(pool):
            nc.gpsimd.memset(ones[:, :], 1.0).then_inc(set_pool, 1)
            with pool.Fori(0, B * PAIRS) as pair:
                for c in range(CHUNKS):
                    base = pair * STEPS + c * TT
                    for s in range(1, POOL_SUMS):
                        pool.wait_ge(exp_done, base + s + 1)
                        if s == 1:
                            if c:
                                pool.wait_ge(acc_used, pair * CHUNKS + c)
                            a, d = prob[:, 0, :, :], prob[:, 1, :, :]
                        else:
                            pool.wait_ge(sum_p, pair * CHUNKS * (POOL_SUMS - 1) + c * (POOL_SUMS - 1) + s - 1)
                            a, d = accp[:, :, :], prob[:, s % RING, :, :]
                        nc.gpsimd.tensor_tensor(accp[:, :, :], a, d, ALU.add).then_inc(sum_p, 1)

        @block.tensor
        def _(pe):
            def transposes(i):
                for g in range(TT // 4):
                    pe.wait_ge(xn_ready, i * (TT // 4) + g + 1)
                    if g >= 2:
                        pe.wait_ge(xT_a, i * (TT // 4) + g - 1)
                        pe.wait_ge(xT_v, i * (TT // 4) + g - 1)
                    for k in range(KT):
                        for t in range(4):
                            last = nc.tensor.transpose(st[:, 2 * (g % 2) + k, 128 * t:128 * t + 128],
                                                       xn[:, g % 2, D * t + 128 * k:D * t + 128 * k + 128], ident[:, :])
                    last.then_inc(tr_ready, 1)

            pe.wait_ge(consts_in, 16 * 7)
            pe.wait_ge(set_v, 1)
            for n in range(2):
                nc.tensor.matmul(st[0:H, n, :], rb[:, 2, :], hot[:, n, :], start=True, stop=True).then_inc(set_pe, 1)
            pe.wait_ge(set_pool, 1)
            pe.wait_ge(set_a, 2)
            with pe.Fori(0, B) as b:
                transposes(2 * b)
                with pe.Fori(0, PAIRS) as hp:
                    pair = b * PAIRS + hp
                    pe.wait_ge(w_in, pair * 48 + 48)
                    pe.wait_ge(xT_a, b * 2 * (TT // 4) + TT // 4)
                    pe.wait_ge(xT_v, b * 2 * (TT // 4) + TT // 4)
                    pe.wait_ge(pair_free, 2 * pair + 2)
                    for n in range(2):
                        for t in range(CHUNKS):
                            f = 4 * n + t
                            if f >= 4:
                                pe.wait_ge(lo_v, pair * 16 + 2 * (f - 3))
                            for k in range(KT):
                                last = nc.tensor.matmul(st[:, f % 4, :], w3[:, n, k, :], xT[:, k, QC * t:QC * t + QC],
                                                        start=(k == 0), stop=(k == KT - 1))
                            last.then_inc(fill, 1)
                    for g in range(4):
                        pe.wait_ge(lo_v, pair * 16 + 8 + 2 * (g + 1))
                        for t in range(4):
                            for k in range(KT):
                                last = nc.tensor.matmul(st[:, g, 128 * t:128 * t + 128],
                                                        xT[:, k, 128 * (4 * g + t):128 * (4 * g + t) + 128], w3[:, 2, k, :],
                                                        start=(t == 0 and k == 0), stop=(t == 3 and k == KT - 1),
                                                        skip_group_check=True)
                        last.then_inc(fill, 1)

                    def scores(n):
                        c, s = divmod(n, TT)
                        j = key_tiles(c)[s]
                        if s == 0:
                            pe.wait_ge(m_in, (pair * CHUNKS + c + 1) * 16)
                        if n >= 2:
                            pe.wait_ge(exp_done, pair * STEPS + n - 1)
                        for h in range(2):
                            o = st[:, 2 * (n % 2) + h, :]
                            nc.tensor.matmul(o, k1[0:MAX_ROW + 1, h, 128 * j:128 * j + 128], q1[0:MAX_ROW + 1, c, h, :],
                                             start=True, stop=False)
                            last = nc.tensor.matmul(o, k2[:, h, 128 * j:128 * j + 128], q2[:, c, h, :],
                                                    start=False, stop=True)
                        last.then_inc(st_ready, 1)

                    def piece(c, u):
                        n = c * PIECES + u
                        t, h, kc = u // 8, u // 4 % 2, u % 4
                        if n >= 2:
                            pe.wait_ge(pre_used, pair * CHUNKS * PIECES + n - 1)
                        o = pre[:, n % 2, :]
                        span = pre_span(QT * c + t, kc)
                        last = nc.tensor.matmul(o, q1[0:MAX_ROW, c, h, 128 * t:128 * t + 128],
                                                k1[0:MAX_ROW, h, 512 * kc:512 * kc + 512], start=True, stop=span is None)
                        if span:
                            lo, hi, at = span
                            last = nc.tensor.matmul(o[:, lo:hi], ident16[:, :], t2[:, h, at:at + hi - lo], start=False, stop=True)
                        last.then_inc(pre_ready, 1)

                    def maxima(c):
                        pe.wait_ge(m_col, pair * CHUNKS + c + 1)
                        if c > 1:
                            pe.wait_ge(rden_done, pair * CHUNKS + c - 1)
                        nc.tensor.transpose(pm[0:2 * QT, 0:128], mcol[:, :], ident[:, :]).then_inc(m_tr, 1)

                    def values(n):
                        c, s = divmod(n, TT)
                        j = key_tiles(c)[s]
                        pe.wait_ge(exp_done, pair * STEPS + n + 1)
                        if s == 0 and c:
                            pe.wait_ge(o_out, pair * CHUNKS + c)
                        for h in range(2):
                            last = nc.tensor.matmul(po[64 * h:64 * h + 64, :], v[:, j, 64 * h:64 * h + 64],
                                                    prob[:, n % RING, h, :], start=(s == 0), stop=(s == TT - 1))
                        last.then_inc(pv_done, 1)

                    def denominators(c):
                        pe.wait_ge(acc_used, pair * CHUNKS + c + 1)
                        pe.wait_ge(m_row, pair * CHUNKS + c + 1)
                        for h in range(2):
                            last = nc.tensor.matmul(pm[64 * h:64 * h + 64, :], ones[:, 0:64], accv[:, h, :], start=True, stop=True)
                        last.then_inc(den_ready, 1)

                    pe.wait_ge(far_set, 2 * pair + 2)
                    pe.wait_ge(t2_cast, pair + 1)
                    pe.wait_ge(hi_a, pair * 16 + 16)
                    for u in range(PIECES):
                        piece(0, u)
                    maxima(0)
                    pe.wait_ge(q_dup, pair * 16 + 16)
                    pe.wait_ge(k_dup, pair * 16 + 16)
                    pe.wait_ge(lo_v, pair * 16 + 16)
                    pe.wait_ge(v_a, pair * 4 + 4)
                    scores(0)
                    for n in range(STEPS):
                        c, s = divmod(n, TT)
                        if n + 1 < STEPS:
                            scores(n + 1)
                        if c + 1 < CHUNKS:
                            for u in pieces_of(s):
                                piece(c + 1, u)
                        values(n)
                        if c and s == 2:
                            denominators(c - 1)
                        if c + 1 < CHUNKS and s == LAST_PRE + 1:
                            maxima(c + 1)
                    denominators(CHUNKS - 1)
                pe.wait_ge(norm_done, (b * PAIRS + PAIRS) * CHUNKS)
                for t in range(TT):
                    if t >= 4:
                        pe.wait_ge(y_out, b * TT + t - 3)
                    for a in range(PAIRS):
                        last = nc.tensor.matmul(st[:, t % 4, 0:D], oT[:, a, 128 * t:128 * t + 128], wo_s[:, a, :],
                                                start=(a == 0), stop=(a == PAIRS - 1))
                    last.then_inc(wo_ready, 1)
                transposes(2 * b + 1)
                pe.wait_ge(gv, b * 11 + 2)
                for k in range(KT):
                    last = nc.tensor.matmul(pm[0:1, 0:E], pooled[:, k:k + 1], gwT[:, k, :], start=(k == 0), stop=(k == KT - 1))
                last.then_inc(g_log, 1)
                pe.wait_ge(gv, b * 11 + 11)
                nc.tensor.matmul(pm[:, 0:E], ones[0:1, :], g1[0:1, 7, :], start=True, stop=True).then_inc(g_bc, 1)
                pe.wait_ge(ew_in, b * 16 + 16)
                pe.wait_ge(xT_a, b * 2 * (TT // 4) + 2 * (TT // 4))
                pe.wait_ge(xT_v, b * 2 * (TT // 4) + 2 * (TT // 4))

                def back(t):
                    pe.wait_ge(ff_acc, b * CHUNKS * E * KT + (t + 1) * E * KT)
                    if t:
                        pe.wait_ge(ft_out, b * CHUNKS + t)
                    for i in range(4):
                        for k in range(KT):
                            last = nc.tensor.transpose(pre[:, i // 2, D * (i % 2) + 128 * k:D * (i % 2) + 128 * k + 128],
                                                       accf[t % 2][:, k, 128 * i:128 * i + 128], ident[:, :])
                    last.then_inc(ft_ready, 1)

                for t in range(CHUNKS):
                    for e in range(E):
                        for o in range(KT):
                            n = (t * E + e) * KT + o
                            if n >= 4:
                                pe.wait_ge(gelu_done, b * CHUNKS * E * KT + n - 3)
                            for k in range(KT):
                                last = nc.tensor.matmul(st[:, n % 4, :], ewT[:, k, D * e + 128 * o:D * e + 128 * o + 128],
                                                        xT[:, k, QC * t:QC * t + QC], start=(k == 0), stop=(k == KT - 1))
                            last.then_inc(ff_ready, 1)
                    if t:
                        back(t - 1)
                back(CHUNKS - 1)

        @block.scalar
        def _(act):
            def ln_sqrt(i):
                act.wait_ge(ln_add, i + 1)
                nc.scalar.activation(std[:, :], std[:, :], ACT.Sqrt).then_inc(ln_sq, 1)

            def xT_out(i):
                for g in range(TT // 4):
                    act.wait_ge(tr_ready, i * (TT // 4) + g + 1)
                    nc.scalar.activation(xT[:, 0, 512 * g:512 * g + 512], st[:, 2 * (g % 2), :], ACT.Copy).then_inc(xT_a, 1)

            act.wait_ge(set_pe, 2)
            for n in range(2):
                nc.scalar.activation(wv_s[:, n, :], st[0:H, n, :], ACT.Copy).then_inc(set_a, 1)
            with act.Fori(0, B) as b:
                ln_sqrt(4 * b)
                xT_out(2 * b)
                with act.Fori(0, PAIRS) as hp:
                    pair = b * PAIRS + hp
                    act.wait_ge(pair_free, 2 * pair + 2)
                    for n in range(2):
                        for t in range(CHUNKS):
                            act.wait_ge(fill, pair * 12 + 4 * n + t + 2)
                            for h in range(2):
                                dst = q1[0:64, t, h, :] if n == 0 else k1[0:64, h, QC * t:QC * t + QC]
                                nc.scalar.activation(dst, st[64 * h:64 * h + 64, t, :], ACT.Copy).then_inc(hi_a, 1)
                    for g in range(4):
                        act.wait_ge(fill, pair * 12 + 8 + g + 2)
                        nc.scalar.activation(v[:, 4 * g:4 * g + 4, :].rearrange("p t d -> p (t d)"), st[:, g, :], ACT.Copy).then_inc(v_a, 1)
                    act.wait_ge(t_in, pair * 32 + 32)
                    nc.scalar.activation(t2[:, :, :], t2f[:, :, :], ACT.Copy).then_inc(t2_cast, 1)

                    def max_row(c):
                        act.wait_ge(m_tr, pair * CHUNKS + c + 1)
                        if c:
                            act.wait_ge(m_in, (pair * CHUNKS + c) * 16)
                        nc.scalar.activation(mrow[:, :], pm[0:2 * QT, 0:128], ACT.Copy, scale=-1.0 / M_UNIT).then_inc(m_row, 1)

                    bands = 0

                    def probs(n, bands):
                        c, s = divmod(n, TT)
                        if band_span(c, key_tiles(c)[s]):
                            bands += 1
                            act.wait_ge(band_in, pair * NBAND + bands)
                        else:
                            act.wait_ge(st_ready, pair * STEPS + n + 1)
                        if n >= RING:
                            m, r = divmod(n - RING, TT)
                            act.wait_ge(pv_done, pair * STEPS + n - RING + 1)
                            if r < POOL_SUMS:
                                act.wait_ge(sum_p, pair * CHUNKS * (POOL_SUMS - 1) + m * (POOL_SUMS - 1) + max(r, 1))
                            else:
                                act.wait_ge(sum_v, pair * CHUNKS * VSUM + m * VSUM + max(r - POOL_SUMS, 1))
                        nc.scalar.activation(prob[:, n % RING, :, :], st[:, 2 * (n % 2):2 * (n % 2) + 2, :], ACT.Exp).then_inc(exp_done, 1)
                        return bands

                    def out_of_psum(c):
                        act.wait_ge(pv_done, pair * STEPS + (c + 1) * TT)
                        nc.scalar.activation(oT[:, bass.ds(hp, 1), QC * c:QC * c + QC], po[:, :], ACT.Copy).then_inc(o_out, 1)

                    max_row(0)
                    bands = probs(0, bands)
                    for n in range(STEPS):
                        c, s = divmod(n, TT)
                        if n + 1 < STEPS:
                            bands = probs(n + 1, bands)
                        if s == TT - 1:
                            out_of_psum(c)
                        if c + 1 < CHUNKS and s == LAST_PRE + 2:
                            max_row(c + 1)
                for t in range(TT):
                    act.wait_ge(wo_ready, b * TT + t + 1)
                    nc.scalar.activation(yb[:, t, :], st[:, t % 4, 0:D], ACT.Copy).then_inc(y_out, 1)
                ln_sqrt(4 * b + 1)
                ln_sqrt(4 * b + 2)
                xT_out(2 * b + 1)
                act.wait_ge(gv, b * 11 + 6)
                nc.scalar.activation(g1[0:1, 5, :], g1[0:1, 1, :], ACT.Exp, bias=g1[0:1, 4, 0:1]).then_inc(g_exp, 1)
                for n in range(CHUNKS * E * KT):
                    e, o = n // KT % E, n % KT
                    act.wait_ge(ff_ready, b * CHUNKS * E * KT + n + 1)
                    if n >= 8:
                        act.wait_ge(ff_acc, b * CHUNKS * E * KT + n - 7)
                    nc.scalar.activation(ge[:, n % 8, :], st[:, n % 4, :], ACT.Gelu, bias=eb[:, KT * e + o:KT * e + o + 1]).then_inc(gelu_done, 1)
                ln_sqrt(4 * b + 3)

        @block.vector
        def _(dve):
            def statistics(i, src):
                for t in range(TT):
                    nc.vector.bn_stats(stats[:, t, :], src[:, t, :]).then_inc(lnv, 1)
                dve.wait_ge(lnv, i * 35 + TT)
                nc.vector.memset(std[:, :], 0.0).then_inc(lnv, 1)
                for t in range(TT):
                    nc.vector.bn_aggr(mv[:, t, :], stats[:, t, :]).then_inc(lnv, 1)
                dve.wait_ge(lnv, i * 35 + 2 * TT + 1)
                nc.vector.tensor_scalar(std[:, :], mv[:, :, 1], EPS, None, ALU.add).then_inc(ln_add, 1)
                dve.wait_ge(ln_sq, i + 1)
                nc.vector.reciprocal(rstd[:, :], std[:, :]).then_inc(lnv, 1)
                dve.wait_ge(lnv, i * 35 + 2 * TT + 2)

            def normalise(i, k):
                for g in range(TT // 4):
                    if g >= 2:
                        dve.wait_ge(tr_ready, k * (TT // 4) + g - 1)
                    for t in range(4):
                        a = 4 * g + t
                        last = nc.vector.tensor_scalar(xn[:, g % 2, D * t:D * t + D], xb[:, a, :], mv[:, a, 0:1], rstd[:, a:a + 1],
                                                       ALU.subtract, ALU.mult)
                    last.then_inc(xn_ready, 1)
                    if g >= 1:
                        xT_half(k, g - 1)
                xT_half(k, TT // 4 - 1)
                dve.wait_ge(xT_v, k * (TT // 4) + TT // 4)
                nc.vector.tensor_copy(g1[0:1, 6, 0:1], rstd[0:1, 0:1]).then_inc(lnv, 1)

            def xT_half(k, g):
                dve.wait_ge(tr_ready, k * (TT // 4) + g + 1)
                nc.vector.tensor_copy(xT[:, 1, 512 * g:512 * g + 512], st[:, 2 * (g % 2) + 1, :]).then_inc(xT_v, 1)

            def residual(i, r, src):
                for t in range(TT):
                    last = nc.vector.tensor_scalar(src[:, t, :], src[:, t, :], mv[:, t, 0:1], rstd[:, t:t + 1], ALU.subtract, ALU.mult)
                last.then_inc(lnv, 1)
                dve.wait_ge(lnv, i * 35 + 2 * TT + 3)
                for t in range(TT):
                    nc.vector.tensor_tensor(xb[:, t, :], xb[:, t, :], src[:, t, :], ALU.add).then_inc(res, 1)
                dve.wait_ge(res, r * TT + TT)

            dve.wait_ge(rel_in, 64)
            dve.wait_ge(consts_in, 16 * 7)
            nc.vector.tensor_tensor(rb[:, 2, :], rb[:, 0, :], rb[:, 1, :], ALU.subtract).then_inc(set_v, 1)
            nc.vector.tensor_tensor(far[64:96, 2, :], far[64:96, 0, :], far[64:96, 1, :], ALU.subtract).then_inc(set_v, 1)
            dve.wait_ge(set_v, 2)
            far16 = q1f[64:96, 0:H]
            nc.vector.tensor_copy(far16, far[64:96, 2, :]).then_inc(set_v, 1)
            dve.wait_ge(set_v, 3)
            nc.vector.tensor_copy(far[64:96, 3, :], far16).then_inc(set_v, 1)
            dve.wait_ge(set_v, 4)
            nc.vector.tensor_tensor(far[64:96, 4, :], far[64:96, 2, :], far[64:96, 3, :], ALU.subtract).then_inc(set_v, 1)
            dve.wait_ge(set_v, 5)
            nc.vector.tensor_scalar(far[64:96, 5, :], far[64:96, 3, :], rowc[64:96, 2, 0:1], None, ALU.mult).then_inc(set_v, 1)
            dve.wait_ge(set_v, 6)
            nc.vector.scalar_tensor_tensor(fparity[64:96, :], far[64:96, 4, :], rowc[64:96, 2, 1:2], far[64:96, 5, :], ALU.mult, ALU.add).then_inc(set_v, 1)
            for h in range(2):
                nc.vector.tensor_copy(k1[64:96, h, :].rearrange("p (t q) -> p t q", q=128),
                                      rowc[64:96, 0, :].unsqueeze(2).broadcast_to((32, TT, 128))).then_inc(set_v, 1)
            nc.vector.memset(k1[MAX_ROW:MAX_ROW + 1, :, :], M_UNIT).then_inc(set_v, 1)
            nc.vector.tensor_copy(ident16[:, :], ident[:, :]).then_inc(set_v, 1)
            dve.wait_ge(set_v, 11)
            nc.vector.tensor_copy(g1[0:1, 6, 0:1], ident[0:1, 0:1]).then_inc(x_free, 1)
            nc.vector.tensor_copy(g1[0:1, 6, 1:2], ident[0:1, 0:1]).then_inc(fill, 1)
            nc.vector.tensor_copy(g1[0:1, 6, 2:3], ident[0:1, 0:1]).then_inc(pair_free, 2)

            with dve.Fori(0, B) as b:
                dve.wait_ge(x_in, b * 16 + 16)
                statistics(4 * b, xb)
                normalise(4 * b, 2 * b)
                with dve.Fori(0, PAIRS) as hp:
                    pair = b * PAIRS + hp
                    for h in range(2):
                        nc.vector.tensor_scalar(q1[64:96, :, h, :].rearrange("p c (t q) -> p c t q", q=128),
                                                rowc[64:96, 1, :].rearrange("p (c t) -> p c t", c=CHUNKS).unsqueeze(3).broadcast_to((32, CHUNKS, QT, 128)),
                                                fparity[64:96, bass.ds(2 * hp + h, 1)], None, ALU.mult).then_inc(far_set, 1)
                    for n in range(2):
                        for t in range(CHUNKS):
                            for h in range(2):
                                dve.wait_ge(hi_a, pair * 16 + 8 * n + 2 * t + h + 1)
                                high = q1[0:64, t, h, :] if n == 0 else k1[0:64, h, QC * t:QC * t + QC]
                                low = q2[64:128, t, h, :] if n == 0 else k2[0:64, h, QC * t:QC * t + QC]
                                nc.vector.tensor_tensor(low, st[64 * h:64 * h + 64, t, :], high, ALU.subtract).then_inc(lo_v, 1)

                    def piece_max(c, u):
                        n = c * PIECES + u
                        t, h, kc = u // 8, u // 4 % 2, u % 4
                        dve.wait_ge(pre_ready, pair * CHUNKS * PIECES + n + 1)
                        nc.vector.reduce_max(mpart[:, h, t, kc:kc + 1], pre[:, n % 2, :], AX.X).then_inc(pre_used, 1)
                        if u == PIECES - 1:
                            dve.wait_ge(pre_used, pair * CHUNKS * PIECES + n + 1)
                            nc.vector.reduce_max(mcol[:, :], mpart[:, :, :, :].rearrange("p h t k -> p (h t) k"), AX.X).then_inc(m_col, 1)

                    def band(n, bands):
                        c, s = divmod(n, TT)
                        span = band_span(c, key_tiles(c)[s])
                        if not span:
                            return bands
                        lo, hi, at = span
                        dve.wait_ge(st_ready, pair * STEPS + n + 1)
                        if bands == 0:
                            dve.wait_ge(t_in, pair * 32 + 32)
                        o = st[:, 2 * (n % 2):2 * (n % 2) + 2, lo:hi]
                        nc.vector.tensor_tensor(o, o, t1[:, :, at:at + hi - lo], ALU.add).then_inc(band_in, 1)
                        return bands + 1

                    def add_probs(n):
                        c, s = divmod(n, TT)
                        k = s - POOL_SUMS
                        if k < 1:
                            return
                        base = pair * CHUNKS * VSUM + c * VSUM
                        dve.wait_ge(exp_done, pair * STEPS + n + 1)
                        if k == 1:
                            if c:
                                dve.wait_ge(den_ready, pair * CHUNKS + c)
                            a = prob[:, (n - 1) % RING, :, :]
                        else:
                            dve.wait_ge(sum_v, base + k - 1)
                            a = accv[:, :, :]
                        nc.vector.tensor_tensor(accv[:, :, :], a, prob[:, n % RING, :, :], ALU.add).then_inc(sum_v, 1)

                    def join(c):
                        dve.wait_ge(sum_v, pair * CHUNKS * VSUM + (c + 1) * VSUM)
                        dve.wait_ge(sum_p, pair * CHUNKS * (POOL_SUMS - 1) + (c + 1) * (POOL_SUMS - 1))
                        nc.vector.tensor_tensor(accv[:, :, :], accv[:, :, :], accp[:, :, :], ALU.add).then_inc(acc_used, 1)

                    def divide(c):
                        dve.wait_ge(den_ready, pair * CHUNKS + c + 1)
                        nc.vector.reciprocal(rden[:, :], pm[:, :]).then_inc(rden_done, 1)
                        dve.wait_ge(rden_done, pair * CHUNKS + c + 1)
                        dve.wait_ge(o_out, pair * CHUNKS + c + 1)
                        o = oT[:, bass.ds(hp, 1), QC * c:QC * c + QC].rearrange("p a q -> p (a q)")
                        nc.vector.tensor_tensor(o, o, rden[:, :], ALU.mult).then_inc(norm_done, 1)

                    dve.wait_ge(far_set, 2 * pair + 2)
                    for u in range(PIECES):
                        piece_max(0, u)
                    bands = band(0, 0)
                    for n in range(STEPS):
                        c, s = divmod(n, TT)
                        if n + 1 < STEPS:
                            bands = band(n + 1, bands)
                        if c + 1 < CHUNKS:
                            for u in pieces_of(s):
                                piece_max(c + 1, u)
                        if n:
                            add_probs(n - 1)
                        if c and s == 1:
                            join(c - 1)
                        if c and s == 3:
                            divide(c - 1)
                    add_probs(STEPS - 1)
                    join(CHUNKS - 1)
                    divide(CHUNKS - 1)
                    dve.wait_ge(norm_done, pair * CHUNKS + CHUNKS)
                    dve.wait_ge(pv_done, pair * STEPS + STEPS)
                    nc.vector.tensor_copy(g1[0:1, 6, 4:5], ident[0:1, 0:1]).then_inc(pair_free, 2)
                dve.wait_ge(y_out, b * TT + TT)
                statistics(4 * b + 1, yb)
                residual(4 * b + 1, 2 * b, yb)
                statistics(4 * b + 2, xb)
                normalise(4 * b + 2, 2 * b + 1)
                dve.wait_ge(xT_a, (2 * b + 2) * (TT // 4))
                for k in range(KT):
                    nc.vector.reduce_sum(pooled[:, k:k + 1], xT[:, k, :], AX.X).then_inc(gv, 1)
                dve.wait_ge(g_log, b + 1)
                nc.vector.scalar_tensor_tensor(g1[0:1, 1, :], pm[0:1, 0:E], 1.0 / S, g1[0:1, 0, :], ALU.mult, ALU.add).then_inc(gv, 1)
                dve.wait_ge(gv, b * 11 + 3)
                nc.vector.tensor_copy(g1[0:1, 3, :], g1[0:1, 1, :]).then_inc(gv, 1)
                nc.vector.max(g1[0:1, 2, :], g1[0:1, 1, :]).then_inc(gv, 1)
                dve.wait_ge(gv, b * 11 + 5)
                nc.vector.tensor_scalar(g1[0:1, 4, 0:1], g1[0:1, 2, 0:1], -1.0, None, ALU.mult).then_inc(gv, 1)
                nc.vector.tensor_scalar(g1[0:1, 3, :], g1[0:1, 1, :], g1[0:1, 2, 1:2], None, ALU.is_ge).then_inc(gv, 1)
                dve.wait_ge(gv, b * 11 + 7)
                dve.wait_ge(g_exp, b + 1)
                nc.vector.tensor_tensor(g1[0:1, 5, :], g1[0:1, 5, :], g1[0:1, 3, :], ALU.mult).then_inc(gv, 1)
                dve.wait_ge(gv, b * 11 + 8)
                nc.vector.reduce_sum(g1[0:1, 4, 1:2], g1[0:1, 5, :], AX.X).then_inc(gv, 1)
                dve.wait_ge(gv, b * 11 + 9)
                nc.vector.reciprocal(g1[0:1, 4, 2:3], g1[0:1, 4, 1:2]).then_inc(gv, 1)
                dve.wait_ge(gv, b * 11 + 10)
                nc.vector.tensor_scalar(g1[0:1, 7, :], g1[0:1, 5, :], g1[0:1, 4, 2:3], None, ALU.mult).then_inc(gv, 1)
                dve.wait_ge(g_bc, b + 1)
                nc.vector.tensor_copy(gate[:, :], pm[:, 0:E]).then_inc(gate_set, 1)
                dve.wait_ge(gate_set, b + 1)

                def ft_copy(t):
                    dve.wait_ge(ft_ready, b * CHUNKS + t + 1)
                    nc.vector.tensor_copy(ft[:, 4 * t:4 * t + 4, :].rearrange("p a d -> p (a d)"),
                                          pre[:, :, :].rearrange("p a n -> p (a n)")).then_inc(ft_out, 1)

                for n in range(CHUNKS * E * KT):
                    t, e, o = n // (KT * E), n // KT % E, n % KT
                    dve.wait_ge(gelu_done, b * CHUNKS * E * KT + n + 1)
                    if e:
                        dve.wait_ge(ff_acc, b * CHUNKS * E * KT + n - KT + 1)
                        nc.vector.scalar_tensor_tensor(accf[t % 2][:, o, :], ge[:, n % 8, :], gate[:, e:e + 1], accf[t % 2][:, o, :],
                                                       ALU.mult, ALU.add).then_inc(ff_acc, 1)
                    else:
                        if t >= 2:
                            dve.wait_ge(ft_ready, b * CHUNKS + t - 1)
                        nc.vector.tensor_scalar(accf[t % 2][:, o, :], ge[:, n % 8, :], gate[:, e:e + 1], None, ALU.mult).then_inc(ff_acc, 1)
                    if t >= 1 and e == E - 1 and o == KT - 1:
                        ft_copy(t - 1)
                ft_copy(CHUNKS - 1)
                dve.wait_ge(ft_out, b * CHUNKS + CHUNKS)
                statistics(4 * b + 3, ft)
                residual(4 * b + 3, 2 * b + 1, ft)


def kernel(L0_attn_hidden_states, L0_attn_wq, L0_attn_wk, L0_attn_wv, L0_attn_wo, L0_attn_rel_bias,
           L0_ffn_gate_w, L0_ffn_gate_b, L0_ffn_expert_w, L0_ffn_expert_b):
    import concourse.bacc as bacc
    from concourse.bass_utils import run_bass_kernel_spmd

    c = np.ascontiguousarray
    onehot, rows, eye = shape_tables()
    ew, eb = np.asarray(L0_ffn_expert_w), np.asarray(L0_ffn_expert_b)
    arrays = {
        "x": c(L0_attn_hidden_states), "wq": c(L0_attn_wq), "wk": c(L0_attn_wk), "wv": c(L0_attn_wv),
        "wo": c(L0_attn_wo), "rel_bias": c(L0_attn_rel_bias),
        "gate_wT": c(np.asarray(L0_ffn_gate_w).T), "gate_b": c(np.asarray(L0_ffn_gate_b).reshape(1, E)),
        "expert_wT": c(ew.reshape(E * D, D).T), "expert_bT": c(eb.reshape(E * KT, 128).T),
        "onehot": onehot, "rows": rows, "eye": eye,
    }
    nc = bacc.Bacc("TRN2", target_bir_lowering=False, num_devices=1)
    aps = [nc.dram_tensor(n, a.shape, mybir.dt.from_np(a.dtype), kind="ExternalInput").ap() for n, a in arrays.items()]
    out = nc.dram_tensor("out", (B, S, D), mybir.dt.float32, kind="ExternalOutput").ap()
    tables = nc.dram_tensor("t_scratch", (2, H, 128, BAND), mybir.dt.float32, kind="Internal").ap()
    scratch = nc.dram_tensor("w_scratch", (H, 2, 512), mybir.dt.float32, kind="Internal").ap()
    layer(nc, *aps, out, scratch, tables)
    r = run_bass_kernel_spmd(nc, [arrays], core_ids=[0])
    return r.results[0]["out"]
```

```python
import numpy as np
import concourse.bass as bass
from concourse import mybir
from contextlib import ExitStack

B, S, D = 2, 2048, 256
H, DK = 16, 64
PAIRS = H // 2
BUCKETS = 32
E = 8
KT = D // 128
TT = S // 128
QC = 512
CHUNKS = S // QC
QT = QC // 128
BAND = 3 * 128
EPS = 1e-5
M_UNIT = 256.0
STEPS = B * CHUNKS * TT
BUCKET_FROM = [0, 1, 2, 3, 4, 5, 6, 7, 8, 12, 16, 23, 32, 46, 64, 91]
MAX_ROW = 96
W_UNIT = 64.0


def key_tiles(c):
    near = [j for j in range(QT * c - 1, QT * c + QT + 1) if 0 <= j < TT]
    return [j for j in range(TT) if j not in near] + near


def band_span(c, j):
    lo, hi = max(128 * (j - 1), QC * c), min(128 * (j + 2), QC * (c + 1))
    return (lo - QC * c, hi - QC * c, lo - 128 * (j - 1)) if lo < hi else None


def pre_span(i, kc):
    lo, hi = max(128 * (i - 1), 512 * kc), min(128 * (i + 2), 512 * (kc + 1))
    return (lo - 512 * kc, hi - 512 * kc, lo - 128 * (i - 1)) if lo < hi else None


PIECES = QT * 2 * 4
PER_STEP = 3
LAST_PRE = (PIECES - 1) // PER_STEP
POOL_SUMS = LAST_PRE + 1
PSUM_P = POOL_SUMS - 1
PSUM_V = TT - POOL_SUMS - 1
RING = 4
SLOTS = B * CHUNKS
FILLS = 3 * 4
G_ALL = SLOTS * PAIRS
FF = E * KT
LN_STEPS = 2 * TT + 7

JOBS = {1: ("proj", 0), 3: ("den", 0), 5: ("proj", 1), 7: ("proj", 2), 10: ("y", 0), 11: ("y", 1), 12: ("max", 0), 14: ("proj", 3)}
DIVIDE_AT = 5


def jobs_of(g):
    out = []
    for s, (kind, n) in sorted(JOBS.items()):
        if kind == "proj":
            if g % CHUNKS == CHUNKS - 1:
                continue
            n += 4 * (g % CHUNKS)
        out.append((s, kind, n))
    return out


def pieces_of(s):
    return range(PER_STEP * s, min(PER_STEP * (s + 1), PIECES)) if s <= LAST_PRE else range(0)


def shape_tables():
    rp = np.arange(-255, 256)
    bucket = np.array([max(n for n in range(16) if BUCKET_FROM[n] <= abs(r)) + 16 * (r > 0) for r in rp])
    hot = (np.arange(BUCKETS)[:, None] == bucket[None, :]).astype(np.float32)
    onehot = np.zeros((BUCKETS, 2, 512), np.float32)
    onehot[:, 0, :511] = hot[:, ::-1]
    onehot[:, 1, :511] = hot
    rows = np.zeros((32, 3, TT), np.float32)
    r, j = np.arange(32)[:, None], np.arange(TT)[None, :]
    rows[:, 0] = j - r // 2 >= 2
    rows[:, 1] = j == r // 2
    rows[:, 2, 0] = np.arange(32) % 2 == 0
    rows[:, 2, 1] = np.arange(32) % 2 == 1
    return onehot, rows, np.eye(128, dtype=np.float32)


def layer(nc, x, w_pairs, wo, rel_bias, gate_wT, gate_b, expert_wT, expert_bT, onehot, rows, eye, out, w_scratch, t_scratch):
    f32, f16 = mybir.dt.float32, mybir.dt.float16
    ACT, ALU, AX = mybir.ActivationFunctionType, mybir.AluOpType, mybir.AxisListType

    ctx = ExitStack()
    with ctx:
        def sb(name, shape, dt):
            return ctx.enter_context(nc.sbuf_tensor(name, shape, dt))

        def pb(name, shape, dt):
            return ctx.enter_context(nc.psum_tensor(name, shape, dt))

        def sem(name):
            return ctx.enter_context(nc.semaphore(name))

        xh = sb("xh", [128, KT, B * S], f16)
        xl = sb("xl", [128, KT, B * S], f16)
        y = sb("y", [128, B * TT, D], f32)
        qk = sb("qk", [128, 16 * S], f16)
        v = sb("v", [128, B, TT, 128], f32)
        prob = sb("prob", [128, RING, 2, QC], f32)
        accv = sb("accv", [128, 2, QC], f32)
        accp = sb("accp", [128, 2, QC], f32)
        o_raw = sb("o_raw", [128, QC], f32)
        rden = sb("rden", [128, QC], f32)
        o_n = sb("o_n", [128, QC], f32)
        t1 = sb("t1", [128, 2, BAND], f32)
        t2f = sb("t2f", [128, 2, BAND], f32)
        t2 = sb("t2", [128, 2, BAND], f16)
        w3 = sb("w3", [128, 3, KT, 128], f32)
        wh = sb("wh", [128, 3, KT, 128], f16)
        wl = sb("wl", [128, 3, KT, 128], f16)
        wo_s = sb("wo_s", [128, PAIRS + 1, D], f32)
        ident = sb("ident", [128, 128], f32)
        ident16 = sb("ident16", [128, 128], f16)
        ones = sb("ones", [128, 128], f32)
        mpart = sb("mpart", [128, 2, QT, 4], f32)
        mcol = sb("mcol", [128, 2 * QT], f32)
        mrow = sb("mrow", [2 * QT, 128], f16)
        rowc = sb("rowc", [96, 3, TT], f32)
        far = sb("far", [96, 6, H], f32)
        far16 = sb("far16", [96, H], f16)
        farv = sb("farv", [96, H + 2], f32)
        rb = sb("rb", [BUCKETS, 3, H], f32)
        stats = sb("stats", [128, TT, 6], f32)
        mv = sb("mv", [128, TT, 2], f32)
        var = sb("var", [128, TT], f32)
        std = sb("std", [128, TT], f32)
        rstd = sb("rstd", [128, TT], f32)
        newton = sb("newton", [128, TT], f32)
        psums = sb("psums", [128, KT, TT // 4], f32)
        pooled = sb("pooled", [128, KT], f32)
        gwT = sb("gwT", [128, KT, E], f32)
        eb = sb("eb", [128, FF], f32)
        g1 = sb("g1", [1, 8, E], f32)
        gate = sb("gate", [128, E], f32)

        def area(n, lo=0, hi=128):
            return qk[lo:hi, 2 * S * n:2 * S * (n + 1)]

        def by_query(n):
            return [area(n + b).rearrange("p (c h q) -> p c h q", c=CHUNKS, h=2) for b in range(B)]

        def by_key(n):
            return [area(n + b).rearrange("p (h s) -> p h s", h=2) for b in range(B)]

        q1 = by_query(0)
        q2 = by_query(2)
        k1 = by_key(4)
        k2 = by_key(6)
        xr = qk[:, 0:8 * S].bitcast(f32).rearrange("p (t d) -> p t d", d=D)
        ewh = area(4).rearrange("p (k n) -> p k n", k=KT)
        ewl = area(5).rearrange("p (k n) -> p k n", k=KT)
        xn = area(6).bitcast(f32).rearrange("p (r n) -> p r n", r=2)
        pflat = prob[:, :, :, :].rearrange("p r h q -> p (r h q)")
        ewf = pflat.rearrange("p (k n) -> p k n", k=KT)
        ge = prob[:, :, :, :].rearrange("p r h q -> p (r h) q")
        hot = pflat[0:BUCKETS, 0:1024].rearrange("p (n u) -> p n u", n=2)
        by_dist = pflat[0:H, 1024:2048].rearrange("p (n u) -> p n u", n=2)
        accf = [accv, accp]

        st = pb("st", [128, 4, 512], f32)
        pre = pb("pre", [128, 2, 512], f32)
        po = pb("po", [128, 512], f32)
        pm = pb("pm", [128, 512], f32)

        consts_in = sem("consts_in")
        rel_in = sem("rel_in")
        set_pool = sem("set_pool")
        set_v = sem("set_v")
        dist_ready = sem("dist_ready")
        dist_out = sem("dist_out")
        scratch_out = sem("scratch_out")
        tables_out = sem("tables_out")
        x_in = [sem(f"x_in{b}") for b in range(B)]
        xr_in = [sem(f"xr_in{b}") for b in range(B)]
        ew_in = sem("ew_in")
        ew_hi = sem("ew_hi")
        ew_lo = sem("ew_lo")
        w_in = sem("w_in")
        w_hi = sem("w_hi")
        w_lo = sem("w_lo")
        t1_in = sem("t1_in")
        t2_in = sem("t2_in")
        t2_cast = sem("t2_cast")
        fill = sem("fill")
        hi_a = sem("hi_a")
        lo_v = sem("lo_v")
        v_a = sem("v_a")
        far_set = sem("far_set")
        q_dup = sem("q_dup")
        k_dup = sem("k_dup")
        pre_ready = sem("pre_ready")
        pre_used = sem("pre_used")
        m_col = sem("m_col")
        m_tr = sem("m_tr")
        m_row = sem("m_row")
        m_in = sem("m_in")
        st_ready = sem("st_ready")
        band_in = sem("band_in")
        exp_done = sem("exp_done")
        pv_done = sem("pv_done")
        o_out = sem("o_out")
        sum_v = sem("sum_v")
        sum_p = sem("sum_p")
        joined = sem("joined")
        den_ready = sem("den_ready")
        den_out = sem("den_out")
        divided = sem("divided")
        y_ready = sem("y_ready")
        y_add = sem("y_add")
        y_zero = sem("y_zero")
        lnv = sem("lnv")
        ln_add = sem("ln_add")
        ln_sq = sem("ln_sq")
        xn_ready = sem("xn_ready")
        tr_ready = sem("tr_ready")
        xh_a = sem("xh_a")
        xl_v = sem("xl_v")
        res = sem("res")
        gv = sem("gv")
        g_log = sem("g_log")
        g_exp = sem("g_exp")
        g_bc = sem("g_bc")
        gate_set = sem("gate_set")
        ff_ready = sem("ff_ready")
        gelu_done = sem("gelu_done")
        ff_acc = sem("ff_acc")
        ft_ready = sem("ft_ready")
        ft_out = sem("ft_out")
        out_done = sem("out_done")

        block = ctx.enter_context(nc.Block())

        NBAND = sum(band_span(c, j) is not None for c in range(CHUNKS) for j in range(TT)) * B
        GROUPS = TT // 4

        def step_of(n):
            g, s = divmod(n % STEPS, TT)
            return g, s, key_tiles(g % CHUNKS)[s]

        def band_of(n):
            g, s, j = step_of(n)
            return band_span(g % CHUNKS, j)

        def sums_before(i, n, pool):
            g, s = divmod(n, TT)
            if pool:
                return (i * SLOTS + g + 1) * PSUM_P + max(s, 1)
            return (i * SLOTS + g + 1) * PSUM_V + max(s - POOL_SUMS, 1)

        @block.sync
        def _(sp):
            for b in range(B):
                sp.dma_start(y[:, TT * b:TT * b + TT, :], x[b, :, :].rearrange("(t p) d -> p t d", p=128)).then_inc(x_in[b], 16)
            sp.dma_start(ident[:, :], eye).then_inc(consts_in, 16)
            sp.dma_start(hot, onehot).then_inc(consts_in, 16)
            sp.dma_start(rowc[64:96, :, :], rows).then_inc(consts_in, 16)
            sp.dma_start(rb[:, 0, :], rel_bias).then_inc(rel_in, 16)
            sp.dma_start(rb[:, 1, :], rel_bias[15:16, :].broadcast_to((BUCKETS, H))).then_inc(rel_in, 16)
            sp.dma_start(far[64:96, 0, :], rel_bias[31:32, :].broadcast_to((32, H))).then_inc(rel_in, 16)
            sp.dma_start(far[64:96, 1, :], rel_bias[15:16, :].broadcast_to((32, H))).then_inc(rel_in, 16)
            sp.dma_start(w3[:, :, :, :].rearrange("p n k c -> p (n k c)"), w_pairs[0, :, :]).then_inc(w_in, 16)
            sp.dma_start(wo_s[:, 1:PAIRS + 1, :], wo.rearrange("(a p) n -> p a n", p=128)).then_inc(consts_in, 16)
            sp.dma_start(gwT[:, :, :], gate_wT.rearrange("(k p) e -> p k e", p=128)).then_inc(consts_in, 16)
            sp.dma_start(eb[:, :], expert_bT).then_inc(consts_in, 16)
            sp.dma_start(g1[0:1, 0, :], gate_b).then_inc(consts_in, 16)
            sp.wait_ge(dist_out, 2)
            sp.dma_start(w_scratch, by_dist).then_inc(scratch_out, 16)
            sp.wait_ge(scratch_out, 16)
            for n in range(2):
                for to, heads in ((0, H), (H, 2)):
                    src = w_scratch[:, n, 127:127 + BAND]
                    src = bass.AP(src.tensor, src.offset, [[1024, heads], [-1, 128], [1, BAND]])
                    sp.dma_start(t_scratch[n, to:to + heads, :, :], src).then_inc(tables_out, 16)
            sp.wait_ge(tables_out, 64)
            sp.dma_start(t2f[:, :, :], t_scratch[1, 0:2, :, :].rearrange("h p u -> p h u")).then_inc(t2_in, 16)

            def duplicates(count, b):
                sp.wait_ge(hi_a, count * 16 + 8)
                sp.dma_start(q2[b][0:64, :, :, :], q1[b][0:64, :, :, :]).then_inc(q_dup, 16)
                sp.wait_ge(hi_a, count * 16 + 16)
                sp.dma_start(k2[b][64:128, :, :], k1[b][0:64, :, :]).then_inc(k_dup, 16)

            def max_in(G, g):
                sp.wait_ge(m_row, G + 1)
                sp.dma_start(q1[g // CHUNKS][MAX_ROW:MAX_ROW + 1, g % CHUNKS, :, :].rearrange("p h (t q) -> p (h t) q", q=128),
                             mrow[:, :]).then_inc(m_in, 16)

            duplicates(0, 0)
            max_in(0, 0)
            with sp.Fori(0, PAIRS) as i:
                sp.wait_ge(band_in, i * NBAND + 1)
                sp.dma_start(t1[:, :, :], t_scratch[0, bass.ds(2 * i, 2), :, :].rearrange("h p u -> p h u")).then_inc(t1_in, 16)
                sp.wait_ge(w_lo, i + 1)
                sp.wait_ge(w_hi, i + 1)
                sp.dma_start(w3[:, :, :, :].rearrange("p n k c -> p (n k c)"),
                             w_pairs[bass.ds(i + 1, 1), :, :].rearrange("a p n -> p (a n)")).then_inc(w_in, 16)
                sp.wait_ge(t2_cast, i + 1)
                sp.dma_start(t2f[:, :, :], t_scratch[1, bass.ds(2 * i + 2, 2), :, :].rearrange("h p u -> p h u")).then_inc(t2_in, 16)
                for g in range(SLOTS):
                    if g % CHUNKS == 2:
                        duplicates(i * B + g // CHUNKS + 1, 1 - g // CHUNKS)
                    max_in(i * SLOTS + g + 1, (g + 1) % SLOTS)
            sp.wait_ge(y_ready, 2 * (G_ALL + 1))
            sp.wait_ge(exp_done, STEPS * PAIRS + 3)
            sp.wait_ge(pv_done, STEPS * PAIRS + RING)
            sp.wait_ge(sum_v, (G_ALL + 1) * PSUM_V)
            sp.wait_ge(sum_p, (G_ALL + 1) * PSUM_P)
            sp.wait_ge(q_dup, 16 * (B * PAIRS + 1))
            sp.wait_ge(m_in, 16 * (G_ALL + 1))
            for b in range(B):
                sp.dma_start(xr[:, TT * b:TT * b + TT, :], x[b, :, :].rearrange("(t p) d -> p t d", p=128)).then_inc(xr_in[b], 16)
                if b == 0:
                    sp.dma_start(ewf, expert_wT.rearrange("(k p) n -> p k n", p=128)).then_inc(ew_in, 16)
            for b in range(B):
                sp.wait_ge(res, (2 * b + 2) * TT)
                sp.dma_start(out[b, :, :].rearrange("(t p) d -> p t d", p=128), xr[:, TT * b:TT * b + TT, :]).then_inc(out_done, 16)
            sp.wait_ge(out_done, 16 * B)

        @block.gpsimd
        def _(pool):
            nc.gpsimd.memset(ones[:, :], 1.0).then_inc(set_pool, 1)
            nc.gpsimd.memset(wo_s[:, 0, :], 0.0).then_inc(set_pool, 1)
            nc.gpsimd.memset(accp[:, :, :], 1.0).then_inc(sum_p, PSUM_P)
            pool.nop().then_inc(divided, 1)

            def divide(G):
                pool.wait_ge(den_out, G + 1)
                pool.wait_ge(o_out, G + 1)
                pool.wait_ge(y_ready, 2 * G + 2)
                nc.gpsimd.tensor_tensor(o_n[:, :], o_raw[:, :], rden[:, :], ALU.mult).then_inc(divided, 1)

            with pool.Fori(0, PAIRS) as i:
                for n in range(STEPS):
                    g, s, _ = step_of(n)
                    G = i * SLOTS + g
                    if 1 <= s < POOL_SUMS:
                        pool.wait_ge(exp_done, i * STEPS + n + 3)
                        if s == 1:
                            pool.wait_ge(joined, G + 1)
                            a, d = prob[:, 0, :, :], prob[:, 1, :, :]
                        else:
                            pool.wait_ge(sum_p, (G + 1) * PSUM_P + s - 1)
                            a, d = accp[:, :, :], prob[:, s % RING, :, :]
                        nc.gpsimd.tensor_tensor(accp[:, :, :], a, d, ALU.add).then_inc(sum_p, 1)
                    if s == DIVIDE_AT:
                        divide(G)
            divide(G_ALL)

        @block.tensor
        def _(pe):
            def transposes(k):
                for g in range(GROUPS):
                    n = k * GROUPS + g
                    pe.wait_ge(xn_ready, n + 1)
                    if n >= 2:
                        pe.wait_ge(xh_a, KT * (n - 1))
                        pe.wait_ge(xl_v, KT * (n - 1))
                    for a in range(KT):
                        for t in range(4):
                            last = nc.tensor.transpose(st[:, 2 * (g % 2) + a, 128 * t:128 * t + 128],
                                                       xn[:, g % 2, D * t + 128 * a:D * t + 128 * a + 128], ident[:, :])
                    last.then_inc(tr_ready, 1)

            def project(b, f, bank):
                if f < 8:
                    cols = slice(S * b + QC * (f % 4), S * b + QC * (f % 4) + QC)
                    terms = [(w[:, f // 4, k, :], t[:, k, cols]) for k in range(KT) for w, t in ((wh, xh), (wl, xh), (wh, xl))]
                    for n, (w, t) in enumerate(terms):
                        last = nc.tensor.matmul(bank, w, t, start=(n == 0), stop=(n == len(terms) - 1))
                else:
                    for t in range(4):
                        at = S * b + 128 * (4 * (f - 8) + t)
                        terms = [(t_[:, k, at:at + 128], w[:, 2, k, :]) for k in range(KT) for w, t_ in ((wh, xh), (wl, xh), (wh, xl))]
                        for n, (t_, w) in enumerate(terms):
                            last = nc.tensor.matmul(bank[:, 128 * t:128 * t + 128], t_, w, start=(n == 0), stop=(n == len(terms) - 1))
                last.then_inc(fill, 1)

            def scores(i, n):
                g, s, j = step_of(n)
                b, c = divmod(g, CHUNKS)
                G = i * SLOTS + n // TT
                if s == 0:
                    pe.wait_ge(m_in, (G + 1) * 16)
                    if c == 0:
                        P = i * B + n // (CHUNKS * TT)
                        pe.wait_ge(q_dup, P * 16 + 16)
                        pe.wait_ge(k_dup, P * 16 + 16)
                        pe.wait_ge(lo_v, P * 16 + 16)
                pe.wait_ge(exp_done, i * STEPS + n + 1)
                for h in range(2):
                    o = st[:, 2 * (n % 2) + h, :]
                    nc.tensor.matmul(o, k1[b][0:MAX_ROW + 1, h, 128 * j:128 * j + 128], q1[b][0:MAX_ROW + 1, c, h, :],
                                     start=True, stop=False)
                    last = nc.tensor.matmul(o, k2[b][:, h, 128 * j:128 * j + 128], q2[b][:, c, h, :], start=False, stop=True)
                last.then_inc(st_ready, 1)

            def piece(G, g, u):
                b, c = divmod(g, CHUNKS)
                t, h, kc = u // 8, u // 4 % 2, u % 4
                pe.wait_ge(pre_used, G * PIECES + u + 1)
                o = pre[:, u % 2, :]
                span = pre_span(QT * c + t, kc)
                last = nc.tensor.matmul(o, q1[b][0:MAX_ROW, c, h, 128 * t:128 * t + 128],
                                        k1[b][0:MAX_ROW, h, 512 * kc:512 * kc + 512], start=True, stop=span is None)
                if span:
                    lo, hi, at = span
                    last = nc.tensor.matmul(o[:, lo:hi], ident16[:, :], t2[:, h, at:at + hi - lo], start=False, stop=True)
                last.then_inc(pre_ready, 1)

            def maxima(G):
                pe.wait_ge(m_col, G + 1)
                nc.tensor.transpose(pm[0:2 * QT, 0:128], mcol[:, :], ident[:, :]).then_inc(m_tr, 1)

            def values(i, n):
                g, s, j = step_of(n)
                pe.wait_ge(exp_done, i * STEPS + n + 3)
                if s == 0:
                    pe.wait_ge(o_out, i * SLOTS + g + 1)
                    if g % CHUNKS == 0:
                        pe.wait_ge(v_a, (i * B + g // CHUNKS) * 4 + 4)
                for h in range(2):
                    last = nc.tensor.matmul(po[64 * h:64 * h + 64, :], v[:, g // CHUNKS, j, 64 * h:64 * h + 64],
                                            prob[:, n % RING, h, :], start=(s == 0), stop=(s == TT - 1))
                last.then_inc(pv_done, 1)

            def denominators(G):
                pe.wait_ge(joined, G + 1)
                for h in range(2):
                    last = nc.tensor.matmul(pm[64 * h:64 * h + 64, :], ones[:, 0:64], accv[:, h, :], start=True, stop=True)
                last.then_inc(den_ready, 1)

            def output(G, n, hp1):
                pe.wait_ge(divided, G + 2)
                for t in range(2):
                    last = nc.tensor.matmul(pm[:, D * t:D * t + D], o_n[:, 128 * (2 * n + t):128 * (2 * n + t) + 128],
                                            wo_s[:, bass.ds(hp1, 1), :].rearrange("p a d -> p (a d)"), start=True, stop=True)
                last.then_inc(y_ready, 1)

            def bank_left(i, g, job):
                s, kind, n = job
                G = i * SLOTS + g
                if kind == "den":
                    pe.wait_ge(den_out, G + 1)
                elif kind == "y":
                    pe.wait_ge(y_add, 2 * G + n + 3)
                elif kind == "max":
                    pe.wait_ge(m_row, G + 2)
                elif n < 8:
                    pe.wait_ge(lo_v, (i * B + g // CHUNKS + 1) * 16 + 2 * n + 2)
                else:
                    pe.wait_ge(v_a, (i * B + g // CHUNKS + 1) * 4 + n - 7)

            pe.nop().then_inc(pv_done, RING)
            pe.nop().then_inc(y_ready, 2)
            pe.wait_ge(consts_in, 16 * 7)
            pe.wait_ge(set_v, 1)
            for n in range(2):
                nc.tensor.matmul(pre[0:H, n, :], rb[:, 2, :], hot[:, n, :], start=True, stop=True).then_inc(dist_ready, 1)
            for b in range(B):
                transposes(b)
            pe.wait_ge(w_hi, 1)
            pe.wait_ge(w_lo, 1)
            pe.wait_ge(xh_a, B * KT * GROUPS)
            pe.wait_ge(xl_v, B * KT * GROUPS)
            for f in range(FILLS):
                if f >= 4:
                    if f < 12:
                        pe.wait_ge(lo_v, 2 * min(f - 3, 8))
                project(0, f, st[:, f % 4, :])
            pe.wait_ge(far_set, 2)
            pe.wait_ge(t2_cast, 1)
            pe.wait_ge(dist_out, 2)
            for u in range(PIECES):
                piece(0, 0, u)
            maxima(0)
            pe.wait_ge(v_a, 4)
            scores(0, 0)
            pe.wait_ge(set_pool, 2)
            with pe.Fori(0, PAIRS) as i:
                before = (SLOTS - 1, jobs_of(SLOTS - 1)[-1])
                for n in range(STEPS):
                    g, s, _ = step_of(n)
                    G = i * SLOTS + g
                    scores(i, n + 1)
                    if s <= LAST_PRE:
                        if s == 0 and g % CHUNKS == CHUNKS - 1:
                            pe.wait_ge(far_set, (i * B + g // CHUNKS + 1) * 2 + 2)
                            pe.wait_ge(hi_a, (i * B + g // CHUNKS + 1) * 16 + 16)
                            if g == SLOTS - 1:
                                pe.wait_ge(t2_cast, i + 2)
                        for u in pieces_of(s):
                            piece(G + 1, (g + 1) % SLOTS, u)
                    values(i, n)
                    for at, kind, k in jobs_of(g):
                        if at != s:
                            continue
                        if before[0] > g:
                            bank_left(i - 1, *before) if before[1][1] != "max" else pe.wait_ge(m_row, G + 1)
                        else:
                            bank_left(i, *before)
                        before = (g, (at, kind, k))
                        if kind == "proj":
                            if k == 0 and g == CHUNKS:
                                pe.wait_ge(w_hi, i + 2)
                                pe.wait_ge(w_lo, i + 2)
                            project(1 - g // CHUNKS, k, pm[:, :])
                        elif kind == "den":
                            denominators(G)
                        elif kind == "y":
                            output(G, k, i if g == 0 else i + 1)
                        else:
                            maxima(G + 1)
            pe.wait_ge(m_row, G_ALL + 1)
            denominators(G_ALL)
            pe.wait_ge(den_out, G_ALL + 1)
            for n in range(2):
                if n:
                    pe.wait_ge(y_add, 2 * G_ALL + 3)
                output(G_ALL, n, PAIRS)
            pe.wait_ge(y_add, 2 * G_ALL + 4)

            def back(b, t):
                n = b * CHUNKS + t
                pe.wait_ge(ff_acc, (n + 1) * FF)
                if n:
                    pe.wait_ge(ft_out, n)
                for a in range(4):
                    for k in range(KT):
                        last = nc.tensor.transpose(pre[:, a // 2, D * (a % 2) + 128 * k:D * (a % 2) + 128 * k + 128],
                                                   accf[t % 2][:, k, 128 * a:128 * a + 128], ident[:, :])
                last.then_inc(ft_ready, 1)

            for b in range(B):
                if b:
                    pe.wait_ge(gelu_done, CHUNKS * FF * b)
                transposes(B + b)
                pe.wait_ge(gv, b * 11 + 2)
                for k in range(KT):
                    last = nc.tensor.matmul(pm[0:1, 0:E], pooled[:, k:k + 1], gwT[:, k, :], start=(k == 0), stop=(k == KT - 1))
                last.then_inc(g_log, 1)
                pe.wait_ge(gv, b * 11 + 11)
                nc.tensor.matmul(pm[:, 0:E], ones[0:1, :], g1[0:1, 7, :], start=True, stop=True).then_inc(g_bc, 1)
                pe.wait_ge(ew_hi, 1)
                pe.wait_ge(ew_lo, 1)
                pe.wait_ge(xh_a, (B + b + 1) * KT * GROUPS)
                pe.wait_ge(xl_v, (B + b + 1) * KT * GROUPS)
                for t in range(CHUNKS):
                    for m in range(FF):
                        n = (b * CHUNKS + t) * FF + m
                        if n >= 4:
                            pe.wait_ge(gelu_done, n - 3)
                        cols = slice(S * b + QC * t, S * b + QC * t + QC)
                        terms = [(w[:, k, 128 * m:128 * m + 128], a[:, k, cols]) for k in range(KT)
                                 for w, a in ((ewh, xh), (ewl, xh), (ewh, xl))]
                        for r, (w, a) in enumerate(terms):
                            last = nc.tensor.matmul(st[:, n % 4, :], w, a, start=(r == 0), stop=(r == len(terms) - 1))
                        last.then_inc(ff_ready, 1)
                    if t:
                        back(b, t - 1)
                back(b, CHUNKS - 1)

        @block.scalar
        def _(act):
            def ln_sqrt(k):
                act.wait_ge(ln_add, k + 1)
                nc.scalar.activation(std[:, :], var[:, :], ACT.Sqrt).then_inc(ln_sq, 1)

            def high_tokens(k):
                for g in range(GROUPS):
                    act.wait_ge(tr_ready, k * GROUPS + g + 1)
                    for a in range(KT):
                        at = S * (k % B) + 512 * g
                        act.activation(xh[:, a, at:at + 512], st[:, 2 * (g % 2) + a, :], ACT.Copy,
                                       accum_out=psums[:, a, g:g + 1]).then_inc(xh_a, 1)

            def split_weights(k):
                act.wait_ge(w_in, 16 * (k + 1))
                nc.scalar.activation(wh[:, :, :, :], w3[:, :, :, :], ACT.Copy, scale=W_UNIT).then_inc(w_hi, 1)

            def high(b, f, bank, P):
                act.wait_ge(fill, P * FILLS + f + 1)
                if f < 8:
                    t = f % 4
                    for h in range(2):
                        dst = q1[b][0:64, t, h, :] if f < 4 else k1[b][0:64, h, QC * t:QC * t + QC]
                        nc.scalar.activation(dst, bank[64 * h:64 * h + 64, :], ACT.Copy, scale=1.0 / W_UNIT).then_inc(hi_a, 1)
                else:
                    nc.scalar.activation(v[:, b, 4 * (f - 8):4 * (f - 8) + 4, :].rearrange("p t d -> p (t d)"), bank,
                                         ACT.Copy, scale=1.0 / W_UNIT).then_inc(v_a, 1)

            def cast_table(k):
                act.wait_ge(t2_in, 16 * (k + 1))
                nc.scalar.activation(t2[:, :, :], t2f[:, :, :], ACT.Copy).then_inc(t2_cast, 1)

            def max_row(G):
                act.wait_ge(m_tr, G + 1)
                nc.scalar.activation(mrow[:, :], pm[0:2 * QT, 0:128], ACT.Copy, scale=-1.0 / M_UNIT).then_inc(m_row, 1)

            def probs(i, n, bands):
                g, s, _ = step_of(n)
                if band_of(n):
                    bands += 1
                    act.wait_ge(band_in, i * NBAND + bands + 1)
                else:
                    act.wait_ge(st_ready, i * STEPS + n + 1)
                act.wait_ge(pv_done, i * STEPS + n + 1)
                was = n - RING
                pool = was % TT < POOL_SUMS
                act.wait_ge(sum_p if pool else sum_v, sums_before(i, was, pool))
                nc.scalar.activation(prob[:, n % RING, :, :], st[:, 2 * (n % 2):2 * (n % 2) + 2, :], ACT.Exp).then_inc(exp_done, 1)
                return bands

            def out_of_psum(i, g):
                act.wait_ge(pv_done, i * STEPS + (g + 1) * TT + RING)
                act.wait_ge(divided, i * SLOTS + g + 2)
                nc.scalar.activation(o_raw[:, :], po[:, :], ACT.Copy).then_inc(o_out, 1)

            act.wait_ge(dist_ready, 2)
            for n in range(2):
                nc.scalar.activation(by_dist[:, n, :], pre[0:H, n, :], ACT.Copy).then_inc(dist_out, 1)
            split_weights(0)
            for b in range(B):
                ln_sqrt(b)
                high_tokens(b)
            for f in range(FILLS):
                high(0, f, st[:, f % 4, :], 0)
                if f == 7:
                    cast_table(0)
            max_row(0)
            act.nop().then_inc(exp_done, 2)
            act.wait_ge(scratch_out, 16)
            probs(0, 0, 0)
            with act.Fori(0, PAIRS) as i:
                bands = 0
                for n in range(STEPS):
                    g, s, _ = step_of(n)
                    G = i * SLOTS + g
                    bands = probs(i, n + 1, bands)
                    if s == TT - 1:
                        out_of_psum(i, g)
                    if s == 0 and g == CHUNKS - 1:
                        split_weights(i + 1)
                    if s == 0 and g == SLOTS - 1:
                        cast_table(i + 1)
                    for at, kind, k in jobs_of(g):
                        if at == s:
                            if kind == "proj":
                                high(1 - g // CHUNKS, k, pm[:, :], i * B + g // CHUNKS + 1)
                            elif kind == "max":
                                max_row(G + 1)
            act.wait_ge(ew_in, 16)
            nc.scalar.activation(ewh, ewf, ACT.Copy, scale=W_UNIT).then_inc(ew_hi, 1)
            for b in range(B):
                ln_sqrt(B + 3 * b)
                ln_sqrt(B + 3 * b + 1)
                high_tokens(B + b)
                act.wait_ge(gv, b * 11 + 6)
                nc.scalar.activation(g1[0:1, 5, :], g1[0:1, 1, :], ACT.Exp, bias=g1[0:1, 4, 0:1]).then_inc(g_exp, 1)
                if b == 0:
                    act.wait_ge(ew_lo, 1)
                for m in range(CHUNKS * FF):
                    n = b * CHUNKS * FF + m
                    act.wait_ge(ff_ready, n + 1)
                    if n >= 8:
                        act.wait_ge(ff_acc, n - 7)
                    nc.scalar.activation(ge[:, n % 8, :], st[:, n % 4, :], ACT.Gelu, bias=eb[:, m % FF:m % FF + 1],
                                         scale=1.0 / W_UNIT).then_inc(gelu_done, 1)
                ln_sqrt(B + 3 * b + 2)

        @block.vector
        def _(dve):
            def statistics(k, src, b):
                base = k * LN_STEPS
                for t in range(TT):
                    nc.vector.bn_stats(stats[:, t, :], src[:, TT * b + t, :]).then_inc(lnv, 1)
                dve.wait_ge(lnv, base + TT)
                for t in range(TT):
                    nc.vector.bn_aggr(mv[:, t, :], stats[:, t, :]).then_inc(lnv, 1)
                dve.wait_ge(lnv, base + 2 * TT)
                nc.vector.tensor_scalar(var[:, :], mv[:, :, 1], EPS, None, ALU.add).then_inc(ln_add, 1)
                dve.wait_ge(ln_sq, k + 1)
                nc.vector.reciprocal(rstd[:, :], std[:, :]).then_inc(lnv, 1)
                dve.wait_ge(lnv, base + 2 * TT + 1)
                nc.vector.tensor_tensor(newton[:, :], rstd[:, :], rstd[:, :], ALU.mult).then_inc(lnv, 1)
                dve.wait_ge(lnv, base + 2 * TT + 2)
                nc.vector.tensor_tensor(newton[:, :], newton[:, :], var[:, :], ALU.mult).then_inc(lnv, 1)
                dve.wait_ge(lnv, base + 2 * TT + 3)
                nc.vector.tensor_scalar(newton[:, :], newton[:, :], -0.5, 1.5, ALU.mult, ALU.add).then_inc(lnv, 1)
                dve.wait_ge(lnv, base + 2 * TT + 4)
                nc.vector.tensor_tensor(rstd[:, :], rstd[:, :], newton[:, :], ALU.mult).then_inc(lnv, 1)
                dve.wait_ge(lnv, base + 2 * TT + 5)

            def low_tokens(k, g):
                for a in range(KT):
                    n = (k * GROUPS + g) * KT + a
                    at = S * (k % B) + 512 * g
                    dve.wait_ge(xh_a, n + 1)
                    nc.vector.tensor_tensor(xl[:, a, at:at + 512], st[:, 2 * (g % 2) + a, :], xh[:, a, at:at + 512],
                                            ALU.subtract).then_inc(xl_v, 1)

            def normalise(k, ln, src, b):
                for g in range(GROUPS):
                    if k * GROUPS + g >= 2:
                        dve.wait_ge(tr_ready, k * GROUPS + g - 1)
                    for t in range(4):
                        a = 4 * g + t
                        last = nc.vector.tensor_scalar(xn[:, g % 2, D * t:D * t + D], src[:, TT * b + a, :], mv[:, a, 0:1],
                                                       rstd[:, a:a + 1], ALU.subtract, ALU.mult)
                    last.then_inc(xn_ready, 1)
                    if g:
                        low_tokens(k, g - 1)
                low_tokens(k, GROUPS - 1)
                dve.wait_ge(xn_ready, (k + 1) * GROUPS)
                nc.vector.memset(g1[0:1, 6, 0:1], 0.0).then_inc(lnv, 1)
                dve.wait_ge(lnv, ln * LN_STEPS + 2 * TT + 6)
                nc.vector.memset(g1[0:1, 6, 1:2], 0.0).then_inc(lnv, 1)

            def residual(ln, r, b):
                for t in range(TT):
                    a = TT * b + t
                    last = nc.vector.tensor_scalar(y[:, a, :], y[:, a, :], mv[:, t, 0:1], rstd[:, t:t + 1], ALU.subtract, ALU.mult)
                last.then_inc(lnv, 1)
                dve.wait_ge(lnv, ln * LN_STEPS + 2 * TT + 6)
                dve.wait_ge(xr_in[b], 16)
                for t in range(TT):
                    a = TT * b + t
                    nc.vector.tensor_tensor(xr[:, a, :], xr[:, a, :], y[:, a, :], ALU.add).then_inc(res, 1)
                dve.wait_ge(res, r * TT + TT)
                nc.vector.memset(g1[0:1, 6, 1:2], 0.0).then_inc(lnv, 1)

            def low_weights(k):
                dve.wait_ge(w_hi, k + 1)
                nc.vector.scalar_tensor_tensor(wl[:, :, :, :], w3[:, :, :, :], W_UNIT, wh[:, :, :, :],
                                               ALU.mult, ALU.subtract).then_inc(w_lo, 1)

            def far_rows(first, b):
                for h in range(2):
                    nc.vector.tensor_scalar(q1[b][64:96, :, h, :].rearrange("p c (t q) -> p c t q", q=128),
                                            rowc[64:96, 1, :].rearrange("p (c t) -> p c t", c=CHUNKS).unsqueeze(3).broadcast_to((32, CHUNKS, QT, 128)),
                                            farv[64:96, bass.ds(first + h, 1)], None, ALU.mult).then_inc(far_set, 1)

            def low(b, f, bank, P):
                t = f % 4
                for h in range(2):
                    dve.wait_ge(hi_a, P * 16 + 2 * f + h + 1)
                    hi = q1[b][0:64, t, h, :] if f < 4 else k1[b][0:64, h, QC * t:QC * t + QC]
                    lo = q2[b][64:128, t, h, :] if f < 4 else k2[b][0:64, h, QC * t:QC * t + QC]
                    nc.vector.scalar_tensor_tensor(lo, bank[64 * h:64 * h + 64, :], 1.0 / W_UNIT, hi,
                                                   ALU.mult, ALU.subtract).then_inc(lo_v, 1)

            def piece_max(G, u):
                t, h, kc = u // 8, u // 4 % 2, u % 4
                dve.wait_ge(pre_ready, G * PIECES + u + 1)
                nc.vector.reduce_max(mpart[:, h, t, kc:kc + 1], pre[:, u % 2, :], AX.X).then_inc(pre_used, 1)
                if u == PIECES - 1:
                    dve.wait_ge(pre_used, G * PIECES + PIECES + 2)
                    nc.vector.reduce_max(mcol[:, :], mpart[:, :, :, :].rearrange("p h t k -> p (h t) k"), AX.X).then_inc(m_col, 1)

            def band(i, n, bands):
                span = band_of(n)
                if not span:
                    return bands
                lo, hi, at = span
                dve.wait_ge(st_ready, i * STEPS + n + 1)
                if bands == 0:
                    dve.wait_ge(t1_in, 16 * (i + 1))
                o = st[:, 2 * (n % 2):2 * (n % 2) + 2, lo:hi]
                nc.vector.tensor_tensor(o, o, t1[:, :, at:at + hi - lo], ALU.add).then_inc(band_in, 1)
                return bands + 1

            def add_probs(i, n):
                g, s, _ = step_of(n)
                k = s - POOL_SUMS
                G = i * SLOTS + g
                if k < 1:
                    return
                dve.wait_ge(exp_done, i * STEPS + n + 3)
                if k == 1:
                    dve.wait_ge(den_ready, G + 1)
                    a = prob[:, (n - 1) % RING, :, :]
                else:
                    dve.wait_ge(sum_v, (G + 1) * PSUM_V + k - 1)
                    a = accv[:, :, :]
                nc.vector.tensor_tensor(accv[:, :, :], a, prob[:, n % RING, :, :], ALU.add).then_inc(sum_v, 1)

            def join(G):
                dve.wait_ge(sum_v, (G + 1) * PSUM_V)
                dve.wait_ge(sum_p, (G + 1) * PSUM_P)
                nc.vector.tensor_tensor(accv[:, :, :], accv[:, :, :], accp[:, :, :], ALU.add).then_inc(joined, 1)

            def invert(G):
                dve.wait_ge(den_ready, G + 1)
                dve.wait_ge(divided, G + 1)
                nc.vector.reciprocal(rden[:, :], pm[:, :]).then_inc(den_out, 1)

            def add_output(G, g, n):
                dve.wait_ge(y_ready, 2 * G + n + 3)
                at = ((g - 1) % SLOTS) * QT + 2 * n
                o = y[:, at:at + 2, :].rearrange("p t d -> p (t d)")
                nc.vector.tensor_tensor(o, o, pm[:, :], ALU.add).then_inc(y_add, 1)

            dve.wait_ge(rel_in, 64)
            dve.wait_ge(consts_in, 16 * 7)
            nc.vector.tensor_tensor(rb[:, 2, :], rb[:, 0, :], rb[:, 1, :], ALU.subtract).then_inc(set_v, 1)
            nc.vector.tensor_tensor(far[64:96, 2, :], far[64:96, 0, :], far[64:96, 1, :], ALU.subtract).then_inc(set_v, 1)
            dve.wait_ge(set_v, 2)
            nc.vector.tensor_copy(far16[64:96, :], far[64:96, 2, :]).then_inc(set_v, 1)
            dve.wait_ge(set_v, 3)
            nc.vector.tensor_copy(far[64:96, 3, :], far16[64:96, :]).then_inc(set_v, 1)
            dve.wait_ge(set_v, 4)
            nc.vector.tensor_tensor(far[64:96, 4, :], far[64:96, 2, :], far[64:96, 3, :], ALU.subtract).then_inc(set_v, 1)
            dve.wait_ge(set_v, 5)
            nc.vector.tensor_scalar(far[64:96, 5, :], far[64:96, 3, :], rowc[64:96, 2, 0:1], None, ALU.mult).then_inc(set_v, 1)
            dve.wait_ge(set_v, 6)
            for to, heads in ((0, H), (H, 2)):
                nc.vector.scalar_tensor_tensor(farv[64:96, to:to + heads], far[64:96, 4, 0:heads], rowc[64:96, 2, 1:2],
                                               far[64:96, 5, 0:heads], ALU.mult, ALU.add).then_inc(set_v, 1)
            nc.vector.tensor_copy(ident16[:, :], ident[:, :]).then_inc(set_v, 1)
            low_weights(0)
            for b in range(B):
                dve.wait_ge(x_in[b], 16)
                statistics(b, y, b)
                normalise(b, b, y, b)
            for b in range(B):
                for h in range(2):
                    nc.vector.tensor_copy(k1[b][64:96, h, :].rearrange("p (t q) -> p t q", q=128),
                                          rowc[64:96, 0, :].unsqueeze(2).broadcast_to((32, TT, 128))).then_inc(set_v, 1)
                nc.vector.memset(k1[b][MAX_ROW:MAX_ROW + 1, :, :], M_UNIT).then_inc(set_v, 1)
            dve.wait_ge(set_v, 9 + 6)
            far_rows(0, 0)
            for f in range(8):
                low(0, f, st[:, f % 4, :], 0)
            dve.wait_ge(lnv, B * LN_STEPS)
            nc.vector.memset(y[:, :, :], 0.0).then_inc(y_zero, 1)
            dve.wait_ge(y_zero, 1)
            nc.vector.memset(accv[:, :, :], 1.0).then_inc(sum_v, PSUM_V)
            nc.vector.memset(o_raw[:, :], 0.0).then_inc(o_out, 1)
            dve.nop().then_inc(y_add, 2)
            dve.nop().then_inc(pre_used, 2)
            dve.nop().then_inc(band_in, 1)
            for u in range(PIECES):
                piece_max(0, u)
            with dve.Fori(0, PAIRS) as i:
                bands = 0
                for n in range(STEPS):
                    g, s, _ = step_of(n)
                    G = i * SLOTS + g
                    bands = band(i, n + 1, bands)
                    for u in pieces_of(s):
                        piece_max(G + 1, u)
                    if s:
                        add_probs(i, n - 1)
                    elif g:
                        add_probs(i, n - 1)
                    if s == TT - 1 and g == SLOTS - 1:
                        add_probs(i, n)
                    if s == 1:
                        join(G)
                    if s == 0 and g == CHUNKS - 1:
                        low_weights(i + 1)
                    for at, kind, k in jobs_of(g):
                        if at == s:
                            if kind == "proj":
                                if k == 0:
                                    dve.wait_ge(fill, (i * B + g // CHUNKS + 1) * FILLS + 1)
                                    far_rows(2 * i + 2 * (g // CHUNKS), 1 - g // CHUNKS)
                                if k < 8:
                                    low(1 - g // CHUNKS, k, pm[:, :], i * B + g // CHUNKS + 1)
                            elif kind == "den":
                                invert(G)
                            elif kind == "y":
                                add_output(G, g, k)
            join(G_ALL)
            invert(G_ALL)
            for n in range(2):
                add_output(G_ALL, 0, n)
            dve.wait_ge(ew_hi, 1)
            nc.vector.scalar_tensor_tensor(ewl, ewf, W_UNIT, ewh, ALU.mult, ALU.subtract).then_inc(ew_lo, 1)
            dve.wait_ge(y_add, 2 * (G_ALL + 2))
            for b in range(B):
                statistics(B + 3 * b, y, b)
                residual(B + 3 * b, 2 * b, b)
                statistics(B + 3 * b + 1, xr, b)
                normalise(B + b, B + 3 * b + 1, xr, b)
                dve.wait_ge(xh_a, (B + b + 1) * KT * GROUPS)
                for k in range(KT):
                    nc.vector.reduce_sum(pooled[:, k:k + 1], psums[:, k, :], AX.X).then_inc(gv, 1)
                dve.wait_ge(g_log, b + 1)
                nc.vector.scalar_tensor_tensor(g1[0:1, 1, :], pm[0:1, 0:E], 1.0 / S, g1[0:1, 0, :], ALU.mult, ALU.add).then_inc(gv, 1)
                dve.wait_ge(gv, b * 11 + 3)
                nc.vector.tensor_copy(g1[0:1, 3, :], g1[0:1, 1, :]).then_inc(gv, 1)
                nc.vector.max(g1[0:1, 2, :], g1[0:1, 1, :]).then_inc(gv, 1)
                dve.wait_ge(gv, b * 11 + 5)
                nc.vector.tensor_scalar(g1[0:1, 4, 0:1], g1[0:1, 2, 0:1], -1.0, None, ALU.mult).then_inc(gv, 1)
                nc.vector.tensor_scalar(g1[0:1, 3, :], g1[0:1, 1, :], g1[0:1, 2, 1:2], None, ALU.is_ge).then_inc(gv, 1)
                dve.wait_ge(gv, b * 11 + 7)
                dve.wait_ge(g_exp, b + 1)
                nc.vector.tensor_tensor(g1[0:1, 5, :], g1[0:1, 5, :], g1[0:1, 3, :], ALU.mult).then_inc(gv, 1)
                dve.wait_ge(gv, b * 11 + 8)
                nc.vector.reduce_sum(g1[0:1, 4, 1:2], g1[0:1, 5, :], AX.X).then_inc(gv, 1)
                dve.wait_ge(gv, b * 11 + 9)
                nc.vector.reciprocal(g1[0:1, 4, 2:3], g1[0:1, 4, 1:2]).then_inc(gv, 1)
                dve.wait_ge(gv, b * 11 + 10)
                nc.vector.tensor_scalar(g1[0:1, 7, :], g1[0:1, 5, :], g1[0:1, 4, 2:3], None, ALU.mult).then_inc(gv, 1)
                dve.wait_ge(g_bc, b + 1)
                nc.vector.tensor_copy(gate[:, :], pm[:, 0:E]).then_inc(gate_set, 1)
                dve.wait_ge(gate_set, b + 1)

                def ft_copy(t):
                    dve.wait_ge(ft_ready, b * CHUNKS + t + 1)
                    nc.vector.tensor_copy(y[:, TT * b + 4 * t:TT * b + 4 * t + 4, :].rearrange("p a d -> p (a d)"),
                                          pre[:, :, :].rearrange("p a n -> p (a n)")).then_inc(ft_out, 1)

                for m in range(CHUNKS * FF):
                    t, e, o = m // FF, m // KT % E, m % KT
                    n = b * CHUNKS * FF + m
                    dve.wait_ge(gelu_done, n + 1)
                    if e:
                        dve.wait_ge(ff_acc, n - KT + 1)
                        nc.vector.scalar_tensor_tensor(accf[t % 2][:, o, :], ge[:, n % 8, :], gate[:, e:e + 1], accf[t % 2][:, o, :],
                                                       ALU.mult, ALU.add).then_inc(ff_acc, 1)
                    else:
                        if b * CHUNKS + t >= 2:
                            dve.wait_ge(ft_ready, b * CHUNKS + t - 1)
                        nc.vector.tensor_scalar(accf[t % 2][:, o, :], ge[:, n % 8, :], gate[:, e:e + 1], None, ALU.mult).then_inc(ff_acc, 1)
                    if t and m % FF == FF - 1:
                        ft_copy(t - 1)
                ft_copy(CHUNKS - 1)
                dve.wait_ge(ft_out, b * CHUNKS + CHUNKS)
                statistics(B + 3 * b + 2, y, b)
                residual(B + 3 * b + 2, 2 * b + 1, b)


def kernel(L0_attn_hidden_states, L0_attn_wq, L0_attn_wk, L0_attn_wv, L0_attn_wo, L0_attn_rel_bias,
           L0_ffn_gate_w, L0_ffn_gate_b, L0_ffn_expert_w, L0_ffn_expert_b):
    import concourse.bacc as bacc
    from concourse.bass_utils import run_bass_kernel_spmd

    c = np.ascontiguousarray
    onehot, rows, eye = shape_tables()
    ew, eb = np.asarray(L0_ffn_expert_w), np.asarray(L0_ffn_expert_b)
    w = np.stack([np.asarray(a).reshape(KT, 128, PAIRS, 128) for a in (L0_attn_wq, L0_attn_wk, L0_attn_wv)])
    w = w.transpose(3, 2, 0, 1, 4).reshape(PAIRS, 128, 3 * KT * 128)
    arrays = {
        "x": c(L0_attn_hidden_states), "w_pairs": c(np.concatenate([w, w[:1]])),
        "wo": c(L0_attn_wo), "rel_bias": c(L0_attn_rel_bias),
        "gate_wT": c(np.asarray(L0_ffn_gate_w).T), "gate_b": c(np.asarray(L0_ffn_gate_b).reshape(1, E)),
        "expert_wT": c(ew.reshape(E * D, D).T), "expert_bT": c(eb.reshape(FF, 128).T),
        "onehot": onehot, "rows": rows, "eye": eye,
    }
    nc = bacc.Bacc("TRN2", target_bir_lowering=False, num_devices=1)
    aps = [nc.dram_tensor(n, a.shape, mybir.dt.from_np(a.dtype), kind="ExternalInput").ap() for n, a in arrays.items()]
    out = nc.dram_tensor("out", (B, S, D), mybir.dt.float32, kind="ExternalOutput").ap()
    tables = nc.dram_tensor("t_scratch", (2, H + 2, 128, BAND), mybir.dt.float32, kind="Internal").ap()
    scratch = nc.dram_tensor("w_scratch", (H, 2, 512), mybir.dt.float32, kind="Internal").ap()
    layer(nc, *aps, out, scratch, tables)
    r = run_bass_kernel_spmd(nc, [arrays], core_ids=[0])
    return r.results[0]["out"]
```

```python
import numpy as np
import concourse.bass as bass
from concourse import mybir
from contextlib import ExitStack

B, S, D = 2, 2048, 256
H, DK = 16, 64
PAIRS = H // 2
BUCKETS = 32
E = 8
KT = D // 128
TT = S // 128
QC = 512
CHUNKS = S // QC
QT = QC // 128
BAND = 3 * 128
EPS = 1e-5
M_UNIT = 256.0
STEPS = B * CHUNKS * TT
BAND_STEPS = [3, 5, 8, 10, 13, 15]
BUCKET_FROM = [0, 1, 2, 3, 4, 5, 6, 7, 8, 12, 16, 23, 32, 46, 64, 91]
MAX_ROW = 96
W_UNIT = 64.0


def key_tiles(c):
    near = [j for j in range(QT * c - 1, QT * c + QT + 1) if 0 <= j < TT]
    order = [j for j in range(TT) if j not in near]
    for n, j in enumerate(near):
        order.insert(BAND_STEPS[n], j)
    return order


def band_span(c, j):
    lo, hi = max(128 * (j - 1), QC * c), min(128 * (j + 2), QC * (c + 1))
    return (lo - QC * c, hi - QC * c, lo - 128 * (j - 1)) if lo < hi else None


def pre_span(i, kc):
    lo, hi = max(128 * (i - 1), 512 * kc), min(128 * (i + 2), 512 * (kc + 1))
    return (lo - 512 * kc, hi - 512 * kc, lo - 128 * (i - 1)) if lo < hi else None


PIECES = QT * 2 * 4
PER_STEP = PIECES // TT
AHEAD = 5
LAST_PRE = TT - 1 - AHEAD
DVE_TILES = [4, 5, 9, 13]
POOL_TILES = [n for n in range(TT) if n not in DVE_TILES]
PSUM_P = len(POOL_TILES) - 1
PSUM_V = len(DVE_TILES) - 1
RING = 4
SLOTS = B * CHUNKS
FILLS = 3 * 4
G_ALL = SLOTS * PAIRS
FF = E * KT
LN_STEPS = 2 * TT + 7

JOBS = {0: ("proj", 0), 2: ("den", 0), 4: ("y", 0), 5: ("y", 1), 6: ("y", 2), 7: ("y", 3), 8: ("proj", 1), 10: ("proj", 2),
        11: ("max", 0), 14: ("proj", 3)}


def piece_of(u):
    return u // 8, u // 2 % 4, u % 2


def jobs_of(g):
    out = []
    for s, (kind, n) in sorted(JOBS.items()):
        if kind == "proj":
            if g % CHUNKS == CHUNKS - 1:
                continue
            n += 4 * (g % CHUNKS)
        out.append((s, kind, n))
    return out


def shape_tables():
    rp = np.arange(-255, 256)
    bucket = np.array([max(n for n in range(16) if BUCKET_FROM[n] <= abs(r)) + 16 * (r > 0) for r in rp])
    hot = (np.arange(BUCKETS)[:, None] == bucket[None, :]).astype(np.float32)
    onehot = np.zeros((BUCKETS, 2, 512), np.float32)
    onehot[:, 0, :511] = hot[:, ::-1]
    onehot[:, 1, :511] = hot
    rows = np.zeros((32, 3, TT), np.float32)
    r, j = np.arange(32)[:, None], np.arange(TT)[None, :]
    rows[:, 0] = j - r // 2 >= 2
    rows[:, 1] = j == r // 2
    rows[:, 2, 0] = np.arange(32) % 2 == 0
    rows[:, 2, 1] = np.arange(32) % 2 == 1
    return onehot, rows, np.eye(128, dtype=np.float32)


def layer(nc, x, w_pairs, wo, rel_bias, gate_wT, gate_b, expert_wT, expert_bT, onehot, rows, eye, out, w_scratch, t_scratch):
    f32, f16 = mybir.dt.float32, mybir.dt.float16
    ACT, ALU, AX = mybir.ActivationFunctionType, mybir.AluOpType, mybir.AxisListType

    ctx = ExitStack()
    with ctx:
        def sb(name, shape, dt):
            return ctx.enter_context(nc.sbuf_tensor(name, shape, dt))

        def pb(name, shape, dt):
            return ctx.enter_context(nc.psum_tensor(name, shape, dt))

        def sem(name):
            return ctx.enter_context(nc.semaphore(name))

        xh = sb("xh", [128, KT, B * S], f16)
        xl = sb("xl", [128, KT, B * S], f16)
        y = sb("y", [128, B * TT, D], f32)
        qk = sb("qk", [128, 16 * S], f16)
        v = sb("v", [128, B, TT, 128], f32)
        prob = sb("prob", [128, RING, 2, QC], f32)
        accv = sb("accv", [128, 2, QC], f32)
        accp = sb("accp", [128, 2, QC], f32)
        o_raw = sb("o_raw", [128, 2, QC], f32)
        rden = sb("rden", [128, 2, QT], f32)
        t1 = sb("t1", [128, 2, BAND], f32)
        t2f = sb("t2f", [128, 2, BAND], f32)
        t2 = sb("t2", [128, 2, BAND], f16)
        w3 = sb("w3", [128, 3, KT, 128], f32)
        wh = sb("wh", [128, 3, KT, 128], f16)
        wl = sb("wl", [128, 3, KT, 128], f16)
        wo_p = [sb(f"wo_p{n}", [128, D], f32) for n in range(2)]
        ident = sb("ident", [128, 128], f32)
        ident16 = sb("ident16", [128, 128], f16)
        ones = sb("ones", [128, 128], f32)
        mpart = sb("mpart", [128, 2 * QT, 4], f32)
        mcol = sb("mcol", [128, 2 * QT], f32)
        mrow = sb("mrow", [2 * QT, 128], f16)
        rowc = sb("rowc", [96, 3, TT], f32)
        far = sb("far", [96, 6, H], f32)
        far16 = sb("far16", [96, H], f16)
        farv = sb("farv", [96, H + 2], f32)
        rb = sb("rb", [BUCKETS, 3, H], f32)
        stats = sb("stats", [128, TT, 6], f32)
        mv = sb("mv", [128, TT, 2], f32)
        var = sb("var", [128, TT], f32)
        std = sb("std", [128, TT], f32)
        rstd = sb("rstd", [128, TT], f32)
        newton = sb("newton", [128, TT], f32)
        psums = sb("psums", [128, KT, TT // 4], f32)
        pooled = sb("pooled", [128, KT], f32)
        gwT = sb("gwT", [128, KT, E], f32)
        eb = sb("eb", [128, FF], f32)
        g1 = sb("g1", [1, 8, E], f32)
        gate = sb("gate", [128, E], f32)

        def area(n, lo=0, hi=128):
            return qk[lo:hi, 2 * S * n:2 * S * (n + 1)]

        def by_query(n):
            return [area(n + b).rearrange("p (c h q) -> p c h q", c=CHUNKS, h=2) for b in range(B)]

        def by_key(n):
            return [area(n + b).rearrange("p (h s) -> p h s", h=2) for b in range(B)]

        q1 = by_query(0)
        q2 = by_query(2)
        k1 = by_key(4)
        k2 = by_key(6)
        xr = qk[:, 0:8 * S].bitcast(f32).rearrange("p (t d) -> p t d", d=D)
        ewh = area(4).rearrange("p (k n) -> p k n", k=KT)
        ewl = area(5).rearrange("p (k n) -> p k n", k=KT)
        xn = area(6).bitcast(f32).rearrange("p (r n) -> p r n", r=2)
        pflat = prob[:, :, :, :].rearrange("p r h q -> p (r h q)")
        ewf = pflat.rearrange("p (k n) -> p k n", k=KT)
        ge = prob[:, :, :, :].rearrange("p r h q -> p (r h) q")
        hot = pflat[0:BUCKETS, 0:1024].rearrange("p (n u) -> p n u", n=2)
        by_dist = pflat[0:H, 1024:2048].rearrange("p (n u) -> p n u", n=2)
        accf = [accv, accp]

        st = pb("st", [128, 4, 512], f32)
        pre = pb("pre", [128, 2, 512], f32)
        po = pb("po", [128, 512], f32)
        pm = pb("pm", [128, 512], f32)

        consts_in = sem("consts_in")
        rel_in = sem("rel_in")
        set_pool = sem("set_pool")
        set_v = sem("set_v")
        dist_ready = sem("dist_ready")
        dist_out = sem("dist_out")
        scratch_out = sem("scratch_out")
        tables_out = sem("tables_out")
        x_in = [sem(f"x_in{b}") for b in range(B)]
        xr_in = [sem(f"xr_in{b}") for b in range(B)]
        ew_in = sem("ew_in")
        ew_hi = sem("ew_hi")
        ew_lo = sem("ew_lo")
        w_in = sem("w_in")
        w_hi = sem("w_hi")
        w_lo = sem("w_lo")
        t1_in = sem("t1_in")
        t2_in = sem("t2_in")
        t2_cast = sem("t2_cast")
        fill = sem("fill")
        hi_a = sem("hi_a")
        lo_v = sem("lo_v")
        v_a = sem("v_a")
        far_set = sem("far_set")
        q_dup = sem("q_dup")
        k_dup = sem("k_dup")
        pre_ready = sem("pre_ready")
        pre_used = sem("pre_used")
        m_col = sem("m_col")
        m_tr = sem("m_tr")
        m_row = sem("m_row")
        m_in = sem("m_in")
        st_ready = sem("st_ready")
        band_in = sem("band_in")
        exp_done = sem("exp_done")
        pv_done = sem("pv_done")
        o_out = sem("o_out")
        sum_v = sem("sum_v")
        sum_p = sem("sum_p")
        joined = sem("joined")
        den_ready = sem("den_ready")
        den_out = sem("den_out")
        wo_in = [sem("wo_in0"), sem("wo_in1")]
        y_ready = sem("y_ready")
        y_add = sem("y_add")
        y_zero = sem("y_zero")
        lnv = sem("lnv")
        ln_add = sem("ln_add")
        ln_sq = sem("ln_sq")
        xn_ready = sem("xn_ready")
        tr_ready = sem("tr_ready")
        xh_a = sem("xh_a")
        xl_v = sem("xl_v")
        res = sem("res")
        gv = sem("gv")
        g_log = sem("g_log")
        g_exp = sem("g_exp")
        g_bc = sem("g_bc")
        gate_set = sem("gate_set")
        ff_ready = sem("ff_ready")
        gelu_done = sem("gelu_done")
        ff_acc = sem("ff_acc")
        ft_ready = sem("ft_ready")
        ft_out = sem("ft_out")
        out_done = sem("out_done")

        block = ctx.enter_context(nc.Block())

        NBAND = sum(band_span(c, j) is not None for c in range(CHUNKS) for j in range(TT)) * B
        GROUPS = TT // 4

        def step_of(n):
            g, s = divmod(n % STEPS, TT)
            return g, s, key_tiles(g % CHUNKS)[s]

        def band_of(n):
            g, s, j = step_of(n)
            return band_span(g % CHUNKS, j)

        def sums_before(i, n):
            g, s = divmod(n, TT)
            mine = DVE_TILES if s in DVE_TILES else POOL_TILES
            return (i * SLOTS + g + 1) * (len(mine) - 1) + max(mine.index(s), 1)

        def pieces_of(g, s):
            return [(1 + (s + AHEAD) // TT, PER_STEP * ((s + AHEAD) % TT) + n) for n in range(PER_STEP)]

        @block.sync
        def _(sp):
            for b in range(B):
                sp.dma_start(y[:, TT * b:TT * b + TT, :], x[b, :, :].rearrange("(t p) d -> p t d", p=128)).then_inc(x_in[b], 16)
            sp.dma_start(ident[:, :], eye).then_inc(consts_in, 16)
            sp.dma_start(hot, onehot).then_inc(consts_in, 16)
            sp.dma_start(rowc[64:96, :, :], rows).then_inc(consts_in, 16)
            sp.dma_start(rb[:, 0, :], rel_bias).then_inc(rel_in, 16)
            sp.dma_start(rb[:, 1, :], rel_bias[15:16, :].broadcast_to((BUCKETS, H))).then_inc(rel_in, 16)
            sp.dma_start(far[64:96, 0, :], rel_bias[31:32, :].broadcast_to((32, H))).then_inc(rel_in, 16)
            sp.dma_start(far[64:96, 1, :], rel_bias[15:16, :].broadcast_to((32, H))).then_inc(rel_in, 16)
            sp.dma_start(w3[:, :, :, :].rearrange("p n k c -> p (n k c)"), w_pairs[0, :, :]).then_inc(w_in, 16)
            sp.dma_start(gwT[:, :, :], gate_wT.rearrange("(k p) e -> p k e", p=128)).then_inc(consts_in, 16)
            sp.dma_start(eb[:, :], expert_bT).then_inc(consts_in, 16)
            sp.dma_start(g1[0:1, 0, :], gate_b).then_inc(consts_in, 16)
            sp.wait_ge(dist_out, 2)
            sp.dma_start(w_scratch, by_dist).then_inc(scratch_out, 16)
            sp.wait_ge(scratch_out, 16)
            for n in range(2):
                for to, heads in ((0, H), (H, 2)):
                    src = w_scratch[:, n, 127:127 + BAND]
                    src = bass.AP(src.tensor, src.offset, [[1024, heads], [-1, 128], [1, BAND]])
                    sp.dma_start(t_scratch[n, to:to + heads, :, :], src).then_inc(tables_out, 16)
            sp.wait_ge(tables_out, 64)
            sp.dma_start(t2f[:, :, :], t_scratch[1, 0:2, :, :].rearrange("h p u -> p h u")).then_inc(t2_in, 16)

            def duplicates(count, b):
                sp.wait_ge(hi_a, count * 16 + 8)
                sp.dma_start(q2[b][0:64, :, :, :], q1[b][0:64, :, :, :]).then_inc(q_dup, 16)
                sp.wait_ge(hi_a, count * 16 + 16)
                sp.dma_start(k2[b][64:128, :, :], k1[b][0:64, :, :]).then_inc(k_dup, 16)

            def max_in(G, g):
                sp.wait_ge(m_row, G + 1)
                sp.dma_start(q1[g // CHUNKS][MAX_ROW:MAX_ROW + 1, g % CHUNKS, :, :].rearrange("p h (t q) -> p (h t) q", q=128),
                             mrow[:, :]).then_inc(m_in, 16)

            duplicates(0, 0)
            max_in(0, 0)
            with sp.Fori(0, PAIRS) as i:
                sp.wait_ge(band_in, i * NBAND + 1)
                sp.dma_start(t1[:, :, :], t_scratch[0, bass.ds(2 * i, 2), :, :].rearrange("h p u -> p h u")).then_inc(t1_in, 16)
                sp.wait_ge(w_lo, i + 1)
                sp.wait_ge(w_hi, i + 1)
                sp.dma_start(w3[:, :, :, :].rearrange("p n k c -> p (n k c)"),
                             w_pairs[bass.ds(i + 1, 1), :, :].rearrange("a p n -> p (a n)")).then_inc(w_in, 16)
                sp.wait_ge(t2_cast, i + 1)
                sp.dma_start(t2f[:, :, :], t_scratch[1, bass.ds(2 * i + 2, 2), :, :].rearrange("h p u -> p h u")).then_inc(t2_in, 16)
                for g in range(SLOTS):
                    if g < 2:
                        sp.wait_ge(y_ready, (i * SLOTS + g) * QT + 1)
                        sp.dma_start(wo_p[g][:, :], wo[bass.ds(i * 128, 128), :]).then_inc(wo_in[g], 16)
                    if g % CHUNKS == 2:
                        duplicates(i * B + g // CHUNKS + 1, 1 - g // CHUNKS)
                    max_in(i * SLOTS + g + 1, (g + 1) % SLOTS)
            sp.wait_ge(y_ready, QT * G_ALL + 1)
            sp.wait_ge(exp_done, STEPS * PAIRS + 4)
            sp.wait_ge(pv_done, STEPS * PAIRS + RING)
            sp.wait_ge(sum_v, (G_ALL + 1) * PSUM_V)
            sp.wait_ge(sum_p, (G_ALL + 1) * PSUM_P)
            sp.wait_ge(q_dup, 16 * (B * PAIRS + 1))
            sp.wait_ge(m_in, 16 * (G_ALL + 1))
            for b in range(B):
                sp.dma_start(xr[:, TT * b:TT * b + TT, :], x[b, :, :].rearrange("(t p) d -> p t d", p=128)).then_inc(xr_in[b], 16)
                if b == 0:
                    sp.dma_start(ewf, expert_wT.rearrange("(k p) n -> p k n", p=128)).then_inc(ew_in, 16)
            for b in range(B):
                sp.wait_ge(res, (2 * b + 2) * TT)
                sp.dma_start(out[b, :, :].rearrange("(t p) d -> p t d", p=128), xr[:, TT * b:TT * b + TT, :]).then_inc(out_done, 16)
            sp.wait_ge(out_done, 16 * B)

        @block.gpsimd
        def _(pool):
            nc.gpsimd.memset(ones[:, :], 1.0).then_inc(set_pool, 1)
            nc.gpsimd.memset(wo_p[1][:, :], 0.0).then_inc(set_pool, 1)
            pool.nop().then_inc(sum_p, PSUM_P)
            with pool.Fori(0, PAIRS) as i:
                for n in range(STEPS):
                    g, s, _ = step_of(n)
                    G = i * SLOTS + g
                    if s in POOL_TILES[1:]:
                        k = POOL_TILES.index(s)
                        pool.wait_ge(exp_done, i * STEPS + n + 3)
                        if k == 1:
                            pool.wait_ge(joined, G + 1)
                            a, d = prob[:, POOL_TILES[0] % RING, :, :], prob[:, s % RING, :, :]
                        else:
                            pool.wait_ge(sum_p, (G + 1) * PSUM_P + k - 1)
                            a, d = accp[:, :, :], prob[:, s % RING, :, :]
                        nc.gpsimd.tensor_tensor(accp[:, :, :], a, d, ALU.add).then_inc(sum_p, 1)
                    if s == TT - 1:
                        pool.wait_ge(sum_p, (G + 2) * PSUM_P)
                        pool.wait_ge(sum_v, (G + 2) * PSUM_V)
                        nc.gpsimd.tensor_tensor(accv[:, :, :], accv[:, :, :], accp[:, :, :], ALU.add).then_inc(joined, 1)

        @block.tensor
        def _(pe):
            def transposes(k):
                for g in range(GROUPS):
                    n = k * GROUPS + g
                    pe.wait_ge(xn_ready, n + 1)
                    if n >= 2:
                        pe.wait_ge(xh_a, KT * (n - 1))
                        pe.wait_ge(xl_v, KT * (n - 1))
                    for a in range(KT):
                        for t in range(4):
                            last = nc.tensor.transpose(st[:, 2 * (g % 2) + a, 128 * t:128 * t + 128],
                                                       xn[:, g % 2, D * t + 128 * a:D * t + 128 * a + 128], ident[:, :])
                    last.then_inc(tr_ready, 1)

            def project(b, f, bank):
                if f < 8:
                    cols = slice(S * b + QC * (f % 4), S * b + QC * (f % 4) + QC)
                    terms = [(w[:, f // 4, k, :], t[:, k, cols]) for k in range(KT) for w, t in ((wh, xh), (wl, xh), (wh, xl))]
                    for n, (w, t) in enumerate(terms):
                        last = nc.tensor.matmul(bank, w, t, start=(n == 0), stop=(n == len(terms) - 1))
                else:
                    for t in range(4):
                        at = S * b + 128 * (4 * (f - 8) + t)
                        terms = [(t_[:, k, at:at + 128], w[:, 2, k, :]) for k in range(KT) for w, t_ in ((wh, xh), (wl, xh), (wh, xl))]
                        for n, (t_, w) in enumerate(terms):
                            last = nc.tensor.matmul(bank[:, 128 * t:128 * t + 128], t_, w, start=(n == 0), stop=(n == len(terms) - 1))
                last.then_inc(fill, 1)

            def scores_wait(i, n):
                g, s, j = step_of(n)
                b, c = divmod(g, CHUNKS)
                G = i * SLOTS + n // TT
                if s == 0:
                    pe.wait_ge(m_in, (G + 1) * 16)
                    if c == 0:
                        P = i * B + n // (CHUNKS * TT)
                        pe.wait_ge(q_dup, P * 16 + 16)
                        pe.wait_ge(k_dup, P * 16 + 16)
                        pe.wait_ge(lo_v, P * 16 + 16)
                pe.wait_ge(exp_done, i * STEPS + n + 1)

            def scores_head(n, h):
                g, s, j = step_of(n)
                b, c = divmod(g, CHUNKS)
                o = st[:, 2 * (n % 2) + h, :]
                nc.tensor.matmul(o, k1[b][0:MAX_ROW + 1, h, 128 * j:128 * j + 128], q1[b][0:MAX_ROW + 1, c, h, :],
                                 start=True, stop=False)
                last = nc.tensor.matmul(o, k2[b][:, h, 128 * j:128 * j + 128], q2[b][:, c, h, :], start=False, stop=True)
                if h == 1:
                    last.then_inc(st_ready, 1)

            def piece(G, g, u):
                b, c = divmod(g, CHUNKS)
                t, kc, h = piece_of(u)
                pe.wait_ge(pre_used, G * PIECES + u + 1)
                o = pre[:, u % 2, :]
                span = pre_span(QT * c + t, kc)
                last = nc.tensor.matmul(o, q1[b][0:MAX_ROW, c, h, 128 * t:128 * t + 128],
                                        k1[b][0:MAX_ROW, h, 512 * kc:512 * kc + 512], start=True, stop=span is None)
                if span:
                    lo, hi, at = span
                    last = nc.tensor.matmul(o[:, lo:hi], ident16[:, :], t2[:, h, at:at + hi - lo], start=False, stop=True)
                last.then_inc(pre_ready, 1)

            def maxima(G):
                pe.wait_ge(m_col, G + 1)
                nc.tensor.transpose(pm[0:2 * QT, 0:128], mcol[:, :], ident[:, :]).then_inc(m_tr, 1)

            def values(i, n):
                g, s, j = step_of(n)
                pe.wait_ge(exp_done, i * STEPS + n + 3)
                if s == 0:
                    pe.wait_ge(o_out, 2 * (i * SLOTS + g) + 2)
                    if g % CHUNKS == 0:
                        pe.wait_ge(v_a, (i * B + g // CHUNKS) * 4 + 4)
                for h in range(2):
                    last = nc.tensor.matmul(po[64 * h:64 * h + 64, :], v[:, g // CHUNKS, j, 64 * h:64 * h + 64],
                                            prob[:, n % RING, h, :], start=(s == 0), stop=(s == TT - 1))
                last.then_inc(pv_done, 1)

            def denominators(G):
                pe.wait_ge(joined, G + 1)
                for h in range(2):
                    for t in range(QT):
                        last = nc.tensor.matmul(pm[:, QT * h + t:QT * h + t + 1], accv[:, h, 128 * t:128 * t + 128], ones[:, 0:1],
                                                start=True, stop=True)
                last.then_inc(den_ready, 1)

            def output(G, t, w, loads):
                if t == 0:
                    pe.wait_ge(o_out, 2 * G + 2)
                    if w == 1:
                        pe.wait_ge(set_pool, 2)
                    if loads is not None:
                        pe.wait_ge(wo_in[w], 16 * loads)
                for h in range(2):
                    last = nc.tensor.matmul(pm[:, D * h:D * h + D], o_raw[:, h, 128 * t:128 * t + 128], wo_p[w][:, :],
                                            start=True, stop=True)
                last.then_inc(y_ready, 1)

            def bank_left(i, g, job):
                s, kind, n = job
                G = i * SLOTS + g
                if kind == "den":
                    pe.wait_ge(den_out, G + 1)
                elif kind == "y":
                    pe.wait_ge(y_add, (G * QT + n + 1) * 2 + 2)
                elif kind == "max":
                    pe.wait_ge(m_row, G + 2)
                elif n < 8:
                    pe.wait_ge(lo_v, (i * B + g // CHUNKS + 1) * 16 + 2 * n + 2)
                else:
                    pe.wait_ge(v_a, (i * B + g // CHUNKS + 1) * 4 + n - 7)

            pe.nop().then_inc(pv_done, RING)
            pe.nop().then_inc(y_ready, 1)
            pe.wait_ge(consts_in, 16 * 6)
            pe.wait_ge(set_v, 1)
            for n in range(2):
                nc.tensor.matmul(pre[0:H, n, :], rb[:, 2, :], hot[:, n, :], start=True, stop=True).then_inc(dist_ready, 1)
            for b in range(B):
                transposes(b)
            pe.wait_ge(w_hi, 1)
            pe.wait_ge(w_lo, 1)
            pe.wait_ge(xh_a, B * KT * GROUPS)
            pe.wait_ge(xl_v, B * KT * GROUPS)
            for f in range(FILLS):
                if f >= 4:
                    if f < 12:
                        pe.wait_ge(lo_v, 2 * min(f - 3, 8))
                project(0, f, st[:, f % 4, :])
            pe.wait_ge(far_set, 2)
            pe.wait_ge(t2_cast, 1)
            pe.wait_ge(dist_out, 2)
            for u in range(PIECES):
                piece(0, 0, u)
            maxima(0)
            pe.wait_ge(v_a, 4)
            for n in range(2):
                scores_wait(0, n)
                for h in range(2):
                    scores_head(n, h)
            for u in range(PER_STEP * AHEAD):
                piece(1, 1, u)
            pe.wait_ge(set_pool, 2)
            with pe.Fori(0, PAIRS) as i:
                before = (SLOTS - 1, jobs_of(SLOTS - 1)[-1])
                for n in range(STEPS):
                    g, s, _ = step_of(n)
                    G = i * SLOTS + g
                    scores_wait(i, n + 2)
                    for h, (ahead, u) in enumerate(pieces_of(g, s)):
                        to = g + ahead
                        scores_head(n + 2, h)
                        if u == 0 and to % CHUNKS == 0:
                            pe.wait_ge(far_set, (i * B + g // CHUNKS + 1) * 2 + 2)
                            pe.wait_ge(hi_a, (i * B + g // CHUNKS + 1) * 16 + 16)
                            if to == SLOTS:
                                pe.wait_ge(t2_cast, i + 2)
                        piece(i * SLOTS + to, to % SLOTS, u)
                    values(i, n)
                    for at, kind, k in jobs_of(g):
                        if at != s:
                            continue
                        if before[0] > g:
                            bank_left(i - 1, *before) if before[1][1] != "max" else pe.wait_ge(m_row, G + 1)
                        else:
                            bank_left(i, *before)
                        before = (g, (at, kind, k))
                        if kind == "proj":
                            if k == 0 and g == CHUNKS:
                                pe.wait_ge(w_hi, i + 2)
                                pe.wait_ge(w_lo, i + 2)
                            project(1 - g // CHUNKS, k, pm[:, :])
                        elif kind == "den":
                            denominators(G)
                        elif kind == "y":
                            output(G, k, 0 if g else 1, (i + 1) if g else None)
                        else:
                            maxima(G + 1)
            pe.wait_ge(m_row, G_ALL + 1)
            denominators(G_ALL)
            pe.wait_ge(den_out, G_ALL + 1)
            pe.wait_ge(wo_in[1], 16 * PAIRS)
            for t in range(QT):
                if t:
                    pe.wait_ge(y_add, (G_ALL * QT + t) * 2 + 2)
                output(G_ALL, t, 1, None)
            pe.wait_ge(y_add, (G_ALL + 1) * QT * 2 + 2)

            def back(b, t):
                n = b * CHUNKS + t
                pe.wait_ge(ff_acc, (n + 1) * FF)
                if n:
                    pe.wait_ge(ft_out, n)
                for a in range(4):
                    for k in range(KT):
                        last = nc.tensor.transpose(pre[:, a // 2, D * (a % 2) + 128 * k:D * (a % 2) + 128 * k + 128],
                                                   accf[t % 2][:, k, 128 * a:128 * a + 128], ident[:, :])
                last.then_inc(ft_ready, 1)

            for b in range(B):
                if b:
                    pe.wait_ge(gelu_done, CHUNKS * FF * b)
                transposes(B + b)
                pe.wait_ge(gv, b * 11 + 2)
                for k in range(KT):
                    last = nc.tensor.matmul(pm[0:1, 0:E], pooled[:, k:k + 1], gwT[:, k, :], start=(k == 0), stop=(k == KT - 1))
                last.then_inc(g_log, 1)
                pe.wait_ge(gv, b * 11 + 11)
                nc.tensor.matmul(pm[:, 0:E], ones[0:1, :], g1[0:1, 7, :], start=True, stop=True).then_inc(g_bc, 1)
                pe.wait_ge(ew_hi, 1)
                pe.wait_ge(ew_lo, 1)
                pe.wait_ge(xh_a, (B + b + 1) * KT * GROUPS)
                pe.wait_ge(xl_v, (B + b + 1) * KT * GROUPS)
                for t in range(CHUNKS):
                    for m in range(FF):
                        n = (b * CHUNKS + t) * FF + m
                        if n >= 4:
                            pe.wait_ge(gelu_done, n - 3)
                        cols = slice(S * b + QC * t, S * b + QC * t + QC)
                        terms = [(w[:, k, 128 * m:128 * m + 128], a[:, k, cols]) for k in range(KT)
                                 for w, a in ((ewh, xh), (ewl, xh), (ewh, xl))]
                        for r, (w, a) in enumerate(terms):
                            last = nc.tensor.matmul(st[:, n % 4, :], w, a, start=(r == 0), stop=(r == len(terms) - 1))
                        last.then_inc(ff_ready, 1)
                    if t:
                        back(b, t - 1)
                back(b, CHUNKS - 1)

        @block.scalar
        def _(act):
            def ln_sqrt(k):
                act.wait_ge(ln_add, k + 1)
                nc.scalar.activation(std[:, :], var[:, :], ACT.Sqrt).then_inc(ln_sq, 1)

            def high_tokens(k):
                for g in range(GROUPS):
                    act.wait_ge(tr_ready, k * GROUPS + g + 1)
                    for a in range(KT):
                        at = S * (k % B) + 512 * g
                        act.activation(xh[:, a, at:at + 512], st[:, 2 * (g % 2) + a, :], ACT.Copy,
                                       accum_out=psums[:, a, g:g + 1]).then_inc(xh_a, 1)

            def split_weights(k):
                act.wait_ge(w_in, 16 * (k + 1))
                nc.scalar.activation(wh[:, :, :, :], w3[:, :, :, :], ACT.Copy, scale=W_UNIT).then_inc(w_hi, 1)

            def high(b, f, bank, P):
                act.wait_ge(fill, P * FILLS + f + 1)
                if f < 8:
                    t = f % 4
                    for h in range(2):
                        dst = q1[b][0:64, t, h, :] if f < 4 else k1[b][0:64, h, QC * t:QC * t + QC]
                        nc.scalar.activation(dst, bank[64 * h:64 * h + 64, :], ACT.Copy, scale=1.0 / W_UNIT).then_inc(hi_a, 1)
                else:
                    nc.scalar.activation(v[:, b, 4 * (f - 8):4 * (f - 8) + 4, :].rearrange("p t d -> p (t d)"), bank,
                                         ACT.Copy, scale=1.0 / W_UNIT).then_inc(v_a, 1)

            def cast_table(k):
                act.wait_ge(t2_in, 16 * (k + 1))
                nc.scalar.activation(t2[:, :, :], t2f[:, :, :], ACT.Copy).then_inc(t2_cast, 1)

            def max_row(G):
                act.wait_ge(m_tr, G + 1)
                nc.scalar.activation(mrow[:, :], pm[0:2 * QT, 0:128], ACT.Copy, scale=-1.0 / M_UNIT).then_inc(m_row, 1)

            def probs(i, n, bands):
                g, s, _ = step_of(n)
                if band_of(n):
                    bands += 1
                    act.wait_ge(band_in, i * NBAND + bands + 1)
                else:
                    act.wait_ge(st_ready, i * STEPS + n + 1)
                act.wait_ge(pv_done, i * STEPS + n + 1)
                was = n - RING
                act.wait_ge(sum_v if was % TT in DVE_TILES else sum_p, sums_before(i, was))
                nc.scalar.activation(prob[:, n % RING, :, :], st[:, 2 * (n % 2):2 * (n % 2) + 2, :], ACT.Exp).then_inc(exp_done, 1)
                return bands

            def out_of_psum(i, g):
                act.wait_ge(pv_done, i * STEPS + (g + 1) * TT + RING)
                act.wait_ge(y_ready, (i * SLOTS + g + 1) * QT + 1)
                for h in range(2):
                    nc.scalar.activation(o_raw[64 * h:64 * h + 64, h, :], po[64 * h:64 * h + 64, :], ACT.Copy).then_inc(o_out, 1)

            act.wait_ge(dist_ready, 2)
            for n in range(2):
                nc.scalar.activation(by_dist[:, n, :], pre[0:H, n, :], ACT.Copy).then_inc(dist_out, 1)
            split_weights(0)
            for b in range(B):
                ln_sqrt(b)
                high_tokens(b)
            for f in range(FILLS):
                high(0, f, st[:, f % 4, :], 0)
                if f == 7:
                    cast_table(0)
            max_row(0)
            act.nop().then_inc(exp_done, 2)
            act.wait_ge(scratch_out, 16)
            for n in range(2):
                probs(0, n, 0)
            with act.Fori(0, PAIRS) as i:
                bands = 0
                for n in range(STEPS):
                    g, s, _ = step_of(n)
                    G = i * SLOTS + g
                    bands = probs(i, n + 2, bands)
                    if s == TT - 1:
                        out_of_psum(i, g)
                    if s == 0 and g == CHUNKS - 1:
                        split_weights(i + 1)
                    if s == LAST_PRE and g == SLOTS - 2:
                        act.wait_ge(pre_ready, (i + 1) * SLOTS * PIECES)
                        cast_table(i + 1)
                    for at, kind, k in jobs_of(g):
                        if at == s:
                            if kind == "proj":
                                high(1 - g // CHUNKS, k, pm[:, :], i * B + g // CHUNKS + 1)
                            elif kind == "max":
                                max_row(G + 1)
            act.wait_ge(ew_in, 16)
            nc.scalar.activation(ewh, ewf, ACT.Copy, scale=W_UNIT).then_inc(ew_hi, 1)
            for b in range(B):
                ln_sqrt(B + 3 * b)
                ln_sqrt(B + 3 * b + 1)
                high_tokens(B + b)
                act.wait_ge(gv, b * 11 + 6)
                nc.scalar.activation(g1[0:1, 5, :], g1[0:1, 1, :], ACT.Exp, bias=g1[0:1, 4, 0:1]).then_inc(g_exp, 1)
                if b == 0:
                    act.wait_ge(ew_lo, 1)
                for m in range(CHUNKS * FF):
                    n = b * CHUNKS * FF + m
                    act.wait_ge(ff_ready, n + 1)
                    if n >= 8:
                        act.wait_ge(ff_acc, n - 7)
                    nc.scalar.activation(ge[:, n % 8, :], st[:, n % 4, :], ACT.Gelu, bias=eb[:, m % FF:m % FF + 1],
                                         scale=1.0 / W_UNIT).then_inc(gelu_done, 1)
                ln_sqrt(B + 3 * b + 2)

        @block.vector
        def _(dve):
            def statistics(k, src, b):
                base = k * LN_STEPS
                for t in range(TT):
                    nc.vector.bn_stats(stats[:, t, :], src[:, TT * b + t, :]).then_inc(lnv, 1)
                dve.wait_ge(lnv, base + TT)
                for t in range(TT):
                    nc.vector.bn_aggr(mv[:, t, :], stats[:, t, :]).then_inc(lnv, 1)
                dve.wait_ge(lnv, base + 2 * TT)
                nc.vector.tensor_scalar(var[:, :], mv[:, :, 1], EPS, None, ALU.add).then_inc(ln_add, 1)
                dve.wait_ge(ln_sq, k + 1)
                nc.vector.reciprocal(rstd[:, :], std[:, :]).then_inc(lnv, 1)
                dve.wait_ge(lnv, base + 2 * TT + 1)
                nc.vector.tensor_tensor(newton[:, :], rstd[:, :], rstd[:, :], ALU.mult).then_inc(lnv, 1)
                dve.wait_ge(lnv, base + 2 * TT + 2)
                nc.vector.tensor_tensor(newton[:, :], newton[:, :], var[:, :], ALU.mult).then_inc(lnv, 1)
                dve.wait_ge(lnv, base + 2 * TT + 3)
                nc.vector.tensor_scalar(newton[:, :], newton[:, :], -0.5, 1.5, ALU.mult, ALU.add).then_inc(lnv, 1)
                dve.wait_ge(lnv, base + 2 * TT + 4)
                nc.vector.tensor_tensor(rstd[:, :], rstd[:, :], newton[:, :], ALU.mult).then_inc(lnv, 1)
                dve.wait_ge(lnv, base + 2 * TT + 5)

            def low_tokens(k, g):
                for a in range(KT):
                    n = (k * GROUPS + g) * KT + a
                    at = S * (k % B) + 512 * g
                    dve.wait_ge(xh_a, n + 1)
                    nc.vector.tensor_tensor(xl[:, a, at:at + 512], st[:, 2 * (g % 2) + a, :], xh[:, a, at:at + 512],
                                            ALU.subtract).then_inc(xl_v, 1)

            def normalise(k, ln, src, b):
                for g in range(GROUPS):
                    if k * GROUPS + g >= 2:
                        dve.wait_ge(tr_ready, k * GROUPS + g - 1)
                    for t in range(4):
                        a = 4 * g + t
                        last = nc.vector.tensor_scalar(xn[:, g % 2, D * t:D * t + D], src[:, TT * b + a, :], mv[:, a, 0:1],
                                                       rstd[:, a:a + 1], ALU.subtract, ALU.mult)
                    last.then_inc(xn_ready, 1)
                    if g:
                        low_tokens(k, g - 1)
                low_tokens(k, GROUPS - 1)
                dve.wait_ge(xn_ready, (k + 1) * GROUPS)
                nc.vector.memset(g1[0:1, 6, 0:1], 0.0).then_inc(lnv, 1)
                dve.wait_ge(lnv, ln * LN_STEPS + 2 * TT + 6)
                nc.vector.memset(g1[0:1, 6, 1:2], 0.0).then_inc(lnv, 1)

            def residual(ln, r, b):
                for t in range(TT):
                    a = TT * b + t
                    last = nc.vector.tensor_scalar(y[:, a, :], y[:, a, :], mv[:, t, 0:1], rstd[:, t:t + 1], ALU.subtract, ALU.mult)
                last.then_inc(lnv, 1)
                dve.wait_ge(lnv, ln * LN_STEPS + 2 * TT + 6)
                dve.wait_ge(xr_in[b], 16)
                for t in range(TT):
                    a = TT * b + t
                    nc.vector.tensor_tensor(xr[:, a, :], xr[:, a, :], y[:, a, :], ALU.add).then_inc(res, 1)
                dve.wait_ge(res, r * TT + TT)
                nc.vector.memset(g1[0:1, 6, 1:2], 0.0).then_inc(lnv, 1)

            def low_weights(k):
                dve.wait_ge(w_hi, k + 1)
                nc.vector.scalar_tensor_tensor(wl[:, :, :, :], w3[:, :, :, :], W_UNIT, wh[:, :, :, :],
                                               ALU.mult, ALU.subtract).then_inc(w_lo, 1)

            def far_rows(first, b):
                for h in range(2):
                    nc.vector.tensor_scalar(q1[b][64:96, :, h, :].rearrange("p c (t q) -> p c t q", q=128),
                                            rowc[64:96, 1, :].rearrange("p (c t) -> p c t", c=CHUNKS).unsqueeze(3).broadcast_to((32, CHUNKS, QT, 128)),
                                            farv[64:96, bass.ds(first + h, 1)], None, ALU.mult).then_inc(far_set, 1)

            def low(b, f, bank, P):
                t = f % 4
                for h in range(2):
                    dve.wait_ge(hi_a, P * 16 + 2 * f + h + 1)
                    hi = q1[b][0:64, t, h, :] if f < 4 else k1[b][0:64, h, QC * t:QC * t + QC]
                    lo = q2[b][64:128, t, h, :] if f < 4 else k2[b][0:64, h, QC * t:QC * t + QC]
                    nc.vector.scalar_tensor_tensor(lo, bank[64 * h:64 * h + 64, :], 1.0 / W_UNIT, hi,
                                                   ALU.mult, ALU.subtract).then_inc(lo_v, 1)

            def piece_max(G, u, first=False):
                t, kc, h = piece_of(u)
                if u == 0 and not first:
                    dve.wait_ge(m_col, G)
                dve.wait_ge(pre_ready, G * PIECES + u + 1)
                nc.vector.reduce_max(mpart[:, QT * h + t, kc:kc + 1], pre[:, u % 2, :], AX.X).then_inc(pre_used, 1)
                if u == PIECES - 1:
                    dve.wait_ge(pre_used, (G + 1) * PIECES + 2)
                    nc.vector.reduce_max(mcol[:, :], mpart[:, :, :], AX.X).then_inc(m_col, 1)

            def band(i, n, bands):
                span = band_of(n)
                if not span:
                    return bands
                lo, hi, at = span
                dve.wait_ge(st_ready, i * STEPS + n + 1)
                if bands == 0:
                    dve.wait_ge(t1_in, 16 * (i + 1))
                o = st[:, 2 * (n % 2):2 * (n % 2) + 2, lo:hi]
                nc.vector.tensor_tensor(o, o, t1[:, :, at:at + hi - lo], ALU.add).then_inc(band_in, 1)
                return bands + 1

            def add_probs(i, n):
                g, s, _ = step_of(n)
                G = i * SLOTS + g
                if s not in DVE_TILES[1:]:
                    return
                k = DVE_TILES.index(s)
                dve.wait_ge(exp_done, i * STEPS + n + 3)
                if k == 1:
                    dve.wait_ge(den_ready, G + 1)
                    a = prob[:, DVE_TILES[0] % RING, :, :]
                else:
                    dve.wait_ge(sum_v, (G + 1) * PSUM_V + k - 1)
                    a = accv[:, :, :]
                nc.vector.tensor_tensor(accv[:, :, :], a, prob[:, n % RING, :, :], ALU.add).then_inc(sum_v, 1)

            def invert(G):
                dve.wait_ge(den_ready, G + 1)
                nc.vector.reciprocal(rden[:, :, :].rearrange("p h t -> p (h t)"), pm[:, 0:2 * QT]).then_inc(den_out, 1)
                dve.wait_ge(den_out, G + 1)

            def add_output(G, g, t):
                at = ((g - 1) % SLOTS) * QT + t
                dve.wait_ge(y_ready, G * QT + t + 2)
                for h in range(2):
                    nc.vector.scalar_tensor_tensor(y[:, at, :], pm[:, D * h:D * h + D], rden[:, h, t:t + 1], y[:, at, :],
                                                   ALU.mult, ALU.add).then_inc(y_add, 1)
                    dve.wait_ge(y_add, (G * QT + t) * 2 + h + 3)

            dve.wait_ge(rel_in, 64)
            dve.wait_ge(consts_in, 16 * 6)
            nc.vector.tensor_tensor(rb[:, 2, :], rb[:, 0, :], rb[:, 1, :], ALU.subtract).then_inc(set_v, 1)
            nc.vector.tensor_tensor(far[64:96, 2, :], far[64:96, 0, :], far[64:96, 1, :], ALU.subtract).then_inc(set_v, 1)
            dve.wait_ge(set_v, 2)
            nc.vector.tensor_copy(far16[64:96, :], far[64:96, 2, :]).then_inc(set_v, 1)
            dve.wait_ge(set_v, 3)
            nc.vector.tensor_copy(far[64:96, 3, :], far16[64:96, :]).then_inc(set_v, 1)
            dve.wait_ge(set_v, 4)
            nc.vector.tensor_tensor(far[64:96, 4, :], far[64:96, 2, :], far[64:96, 3, :], ALU.subtract).then_inc(set_v, 1)
            dve.wait_ge(set_v, 5)
            nc.vector.tensor_scalar(far[64:96, 5, :], far[64:96, 3, :], rowc[64:96, 2, 0:1], None, ALU.mult).then_inc(set_v, 1)
            dve.wait_ge(set_v, 6)
            for to, heads in ((0, H), (H, 2)):
                nc.vector.scalar_tensor_tensor(farv[64:96, to:to + heads], far[64:96, 4, 0:heads], rowc[64:96, 2, 1:2],
                                               far[64:96, 5, 0:heads], ALU.mult, ALU.add).then_inc(set_v, 1)
            nc.vector.tensor_copy(ident16[:, :], ident[:, :]).then_inc(set_v, 1)
            low_weights(0)
            for b in range(B):
                dve.wait_ge(x_in[b], 16)
                statistics(b, y, b)
                normalise(b, b, y, b)
            for b in range(B):
                for h in range(2):
                    nc.vector.tensor_copy(k1[b][64:96, h, :].rearrange("p (t q) -> p t q", q=128),
                                          rowc[64:96, 0, :].unsqueeze(2).broadcast_to((32, TT, 128))).then_inc(set_v, 1)
                nc.vector.memset(k1[b][MAX_ROW:MAX_ROW + 1, :, :], M_UNIT).then_inc(set_v, 1)
            dve.wait_ge(set_v, 9 + 6)
            far_rows(0, 0)
            for f in range(8):
                low(0, f, st[:, f % 4, :], 0)
            dve.wait_ge(lnv, B * LN_STEPS)
            nc.vector.memset(y[:, :, :], 0.0).then_inc(y_zero, 1)
            dve.wait_ge(y_zero, 1)
            nc.vector.memset(accv[:, :, :], 1.0).then_inc(joined, 1)
            dve.nop().then_inc(sum_v, PSUM_V)
            nc.vector.memset(o_raw[:, :, :], 0.0).then_inc(o_out, 2)
            dve.nop().then_inc(y_add, 2)
            dve.nop().then_inc(pre_used, 2)
            dve.nop().then_inc(band_in, 1)
            for u in range(PIECES):
                piece_max(0, u, first=True)
            for u in range(PER_STEP * AHEAD):
                piece_max(1, u)
            with dve.Fori(0, PAIRS) as i:
                bands = 0
                for n in range(STEPS):
                    g, s, _ = step_of(n)
                    G = i * SLOTS + g
                    (ahead, u), (ahead2, u2) = pieces_of(g, s)
                    piece_max(G + ahead, u)
                    bands = band(i, n + 2, bands)
                    piece_max(G + ahead2, u2)
                    add_probs(i, n)
                    if s == 0 and g == CHUNKS - 1:
                        low_weights(i + 1)
                    for at, kind, k in jobs_of(g):
                        if at == s:
                            if kind == "proj":
                                if k == 0:
                                    dve.wait_ge(fill, (i * B + g // CHUNKS + 1) * FILLS + 1)
                                    far_rows(2 * i + 2 * (g // CHUNKS), 1 - g // CHUNKS)
                                if k < 8:
                                    low(1 - g // CHUNKS, k, pm[:, :], i * B + g // CHUNKS + 1)
                            elif kind == "den":
                                invert(G)
                            elif kind == "y":
                                add_output(G, g, k)
            invert(G_ALL)
            for t in range(QT):
                add_output(G_ALL, 0, t)
            dve.wait_ge(ew_hi, 1)
            nc.vector.scalar_tensor_tensor(ewl, ewf, W_UNIT, ewh, ALU.mult, ALU.subtract).then_inc(ew_lo, 1)
            dve.wait_ge(y_add, (G_ALL + 1) * QT * 2 + 2)
            for b in range(B):
                statistics(B + 3 * b, y, b)
                residual(B + 3 * b, 2 * b, b)
                statistics(B + 3 * b + 1, xr, b)
                normalise(B + b, B + 3 * b + 1, xr, b)
                dve.wait_ge(xh_a, (B + b + 1) * KT * GROUPS)
                for k in range(KT):
                    nc.vector.reduce_sum(pooled[:, k:k + 1], psums[:, k, :], AX.X).then_inc(gv, 1)
                dve.wait_ge(g_log, b + 1)
                nc.vector.scalar_tensor_tensor(g1[0:1, 1, :], pm[0:1, 0:E], 1.0 / S, g1[0:1, 0, :], ALU.mult, ALU.add).then_inc(gv, 1)
                dve.wait_ge(gv, b * 11 + 3)
                nc.vector.tensor_copy(g1[0:1, 3, :], g1[0:1, 1, :]).then_inc(gv, 1)
                nc.vector.max(g1[0:1, 2, :], g1[0:1, 1, :]).then_inc(gv, 1)
                dve.wait_ge(gv, b * 11 + 5)
                nc.vector.tensor_scalar(g1[0:1, 4, 0:1], g1[0:1, 2, 0:1], -1.0, None, ALU.mult).then_inc(gv, 1)
                nc.vector.tensor_scalar(g1[0:1, 3, :], g1[0:1, 1, :], g1[0:1, 2, 1:2], None, ALU.is_ge).then_inc(gv, 1)
                dve.wait_ge(gv, b * 11 + 7)
                dve.wait_ge(g_exp, b + 1)
                nc.vector.tensor_tensor(g1[0:1, 5, :], g1[0:1, 5, :], g1[0:1, 3, :], ALU.mult).then_inc(gv, 1)
                dve.wait_ge(gv, b * 11 + 8)
                nc.vector.reduce_sum(g1[0:1, 4, 1:2], g1[0:1, 5, :], AX.X).then_inc(gv, 1)
                dve.wait_ge(gv, b * 11 + 9)
                nc.vector.reciprocal(g1[0:1, 4, 2:3], g1[0:1, 4, 1:2]).then_inc(gv, 1)
                dve.wait_ge(gv, b * 11 + 10)
                nc.vector.tensor_scalar(g1[0:1, 7, :], g1[0:1, 5, :], g1[0:1, 4, 2:3], None, ALU.mult).then_inc(gv, 1)
                dve.wait_ge(g_bc, b + 1)
                nc.vector.tensor_copy(gate[:, :], pm[:, 0:E]).then_inc(gate_set, 1)
                dve.wait_ge(gate_set, b + 1)

                def ft_copy(t):
                    dve.wait_ge(ft_ready, b * CHUNKS + t + 1)
                    nc.vector.tensor_copy(y[:, TT * b + 4 * t:TT * b + 4 * t + 4, :].rearrange("p a d -> p (a d)"),
                                          pre[:, :, :].rearrange("p a n -> p (a n)")).then_inc(ft_out, 1)

                for m in range(CHUNKS * FF):
                    t, e, o = m // FF, m // KT % E, m % KT
                    n = b * CHUNKS * FF + m
                    dve.wait_ge(gelu_done, n + 1)
                    if e:
                        dve.wait_ge(ff_acc, n - KT + 1)
                        nc.vector.scalar_tensor_tensor(accf[t % 2][:, o, :], ge[:, n % 8, :], gate[:, e:e + 1], accf[t % 2][:, o, :],
                                                       ALU.mult, ALU.add).then_inc(ff_acc, 1)
                    else:
                        if b * CHUNKS + t >= 2:
                            dve.wait_ge(ft_ready, b * CHUNKS + t - 1)
                        nc.vector.tensor_scalar(accf[t % 2][:, o, :], ge[:, n % 8, :], gate[:, e:e + 1], None, ALU.mult).then_inc(ff_acc, 1)
                    if t and m % FF == FF - 1:
                        ft_copy(t - 1)
                ft_copy(CHUNKS - 1)
                dve.wait_ge(ft_out, b * CHUNKS + CHUNKS)
                statistics(B + 3 * b + 2, y, b)
                residual(B + 3 * b + 2, 2 * b + 1, b)


def kernel(L0_attn_hidden_states, L0_attn_wq, L0_attn_wk, L0_attn_wv, L0_attn_wo, L0_attn_rel_bias,
           L0_ffn_gate_w, L0_ffn_gate_b, L0_ffn_expert_w, L0_ffn_expert_b):
    import concourse.bacc as bacc
    from concourse.bass_utils import run_bass_kernel_spmd

    c = np.ascontiguousarray
    onehot, rows, eye = shape_tables()
    ew, eb = np.asarray(L0_ffn_expert_w), np.asarray(L0_ffn_expert_b)
    w = np.stack([np.asarray(a).reshape(KT, 128, PAIRS, 128) for a in (L0_attn_wq, L0_attn_wk, L0_attn_wv)])
    w = w.transpose(3, 2, 0, 1, 4).reshape(PAIRS, 128, 3 * KT * 128)
    arrays = {
        "x": c(L0_attn_hidden_states), "w_pairs": c(np.concatenate([w, w[:1]])),
        "wo": c(L0_attn_wo), "rel_bias": c(L0_attn_rel_bias),
        "gate_wT": c(np.asarray(L0_ffn_gate_w).T), "gate_b": c(np.asarray(L0_ffn_gate_b).reshape(1, E)),
        "expert_wT": c(ew.reshape(E * D, D).T), "expert_bT": c(eb.reshape(FF, 128).T),
        "onehot": onehot, "rows": rows, "eye": eye,
    }
    nc = bacc.Bacc("TRN2", target_bir_lowering=False, num_devices=1)
    aps = [nc.dram_tensor(n, a.shape, mybir.dt.from_np(a.dtype), kind="ExternalInput").ap() for n, a in arrays.items()]
    out = nc.dram_tensor("out", (B, S, D), mybir.dt.float32, kind="ExternalOutput").ap()
    tables = nc.dram_tensor("t_scratch", (2, H + 2, 128, BAND), mybir.dt.float32, kind="Internal").ap()
    scratch = nc.dram_tensor("w_scratch", (H, 2, 512), mybir.dt.float32, kind="Internal").ap()
    layer(nc, *aps, out, scratch, tables)
    r = run_bass_kernel_spmd(nc, [arrays], core_ids=[0])
    return r.results[0]["out"]
```
